# Optimizing a Trainium2 kernel written in Bass

```python
import numpy as np
import jax
import jax.numpy as jnp

def _softmax(x, axis=-1):
    return jax.nn.softmax(x, axis=axis)

def _gelu(x):
    return jax.nn.gelu(x, approximate=True)

def _silu(x):
    return jax.nn.silu(x)

def _sigmoid(x):
    return jax.nn.sigmoid(x)

def _layernorm(x, axis=-1, eps=1e-05):
    m = jnp.mean(x, axis=axis, keepdims=True)
    v = jnp.var(x, axis=axis, keepdims=True)
    return (x - m) / jnp.sqrt(v + eps)

def _scatter_add(tgt, idx, src, axis=0):
    return tgt.at[idx].add(src)

def _segment_sum(src, seg, n):
    return jax.ops.segment_sum(src, seg, n)
kernel_name = 'mk_perceiver_d1_seqx_r8_e53472'

def setup_inputs(seed: int=0):
    np.random.seed(seed)
    _w = jnp.asarray

    def _rec_inputs():
        import jax
        import jax.numpy as jnp
        _rk = jax.random.key(seed)
        x = 7.22e-05 + 1 * jax.random.normal(jax.random.fold_in(_rk, 1), (32, 64, 128), jnp.float32)
        _lenS = 64 - jax.random.randint(jax.random.fold_in(_rk, 7), (32,), 0, max(1, 64 // 4) + 1, jnp.int32)
        _lenS2 = 1601 - jax.random.randint(jax.random.fold_in(_rk, 8), (32,), 0, max(1, 1601 // 4) + 1, jnp.int32)
        _ctx_1024P = jax.random.normal(jax.random.fold_in(_rk, 11), (32, 16, 128), jnp.float32)
        _ctx_1024c = jax.random.dirichlet(jax.random.fold_in(_rk, 511), 0.3 * jnp.ones((16,), jnp.float32), (32, 1601))
        _ctx_1024t = jnp.einsum('bsk,bkd->bsd', _ctx_1024c, _ctx_1024P)
        _ctx_1024t = _ctx_1024t * jax.lax.rsqrt(jnp.mean(jnp.square(_ctx_1024t)) + 1e-12) * 0.953939
        ctx_1024 = 4.13588e-05 + 0.999923 * (_ctx_1024t + 0.3 * jax.random.normal(jax.random.fold_in(_rk, 611), (32, 1601, 128), jnp.float32))
        return (x, ctx_1024)
    x, ctx_1024 = _rec_inputs()

    def _L0_xattn_setup():
        import jax, jax.numpy as jnp
        import numpy as np
        EMBED = 128
        HEADS = 16
        HEAD_DIM = EMBED // HEADS
        key = jax.random.key(seed)
        ks = jax.random.split(key, 10)
        B, N, M = (4, 256, 256)
        s = 1.0 / np.sqrt(EMBED)
        return {'xq': jax.random.normal(ks[0], (B, N, EMBED), jnp.float32), 'xk': jax.random.normal(ks[1], (B, M, EMBED), jnp.float32), 'xv': jax.random.normal(ks[2], (B, M, EMBED), jnp.float32), 'Wq': jax.random.normal(ks[3], (EMBED, EMBED), jnp.float32) * s, 'bq': jnp.zeros((EMBED,), jnp.float32), 'Wk': jax.random.normal(ks[4], (EMBED, EMBED), jnp.float32) * s, 'bk': jnp.zeros((EMBED,), jnp.float32), 'Wv': jax.random.normal(ks[5], (EMBED, EMBED), jnp.float32) * s, 'bv': jnp.zeros((EMBED,), jnp.float32), 'Wo': jax.random.normal(ks[6], (EMBED, EMBED), jnp.float32) * s}
    _L0_xattn_all = _L0_xattn_setup()
    _L0_xattn_in = {k: v for k, v in _L0_xattn_all.items() if k in ('Wq', 'bq', 'Wk', 'bk', 'Wv', 'bv', 'Wo')}
    del _L0_xattn_all

    def _L0_attn_setup():
        import jax, jax.numpy as jnp
        import numpy as np
        B, N, C = (2, 256, 128)
        H = 16
        HD = C // H
        R = 16
        LORA_SCALE = 32.0 / R
        ATTN_SCALE = HD ** (-0.5)
        key = jax.random.key(seed)
        ks = jax.random.split(key, 10)
        s = lambda fan_in: 1.0 / np.sqrt(fan_in)
        return {'x': jax.random.normal(ks[0], (B, N, C), dtype=jnp.float32), 'w_qkv': jax.random.normal(ks[1], (C, 3 * C), dtype=jnp.float32) * s(C), 'b_qkv': jax.random.normal(ks[2], (3 * C,), dtype=jnp.float32) * 0.02, 'a_q': jax.random.normal(ks[3], (HD, R), dtype=jnp.float32) * s(HD), 'b_q': jax.random.normal(ks[4], (R, HD), dtype=jnp.float32) * 0.02, 'a_v': jax.random.normal(ks[5], (HD, R), dtype=jnp.float32) * s(HD), 'b_v': jax.random.normal(ks[6], (R, HD), dtype=jnp.float32) * 0.02, 'w_proj': jax.random.normal(ks[7], (C, C), dtype=jnp.float32) * s(C), 'b_proj': jax.random.normal(ks[8], (C,), dtype=jnp.float32) * 0.02}
    _L0_attn_all = _L0_attn_setup()
    _L0_attn_in = {k: v for k, v in _L0_attn_all.items() if k in ('w_qkv', 'b_qkv', 'a_q', 'b_q', 'a_v', 'b_v', 'w_proj', 'b_proj')}
    del _L0_attn_all

    def _L0_ffn_setup():
        import jax, jax.numpy as jnp
        import numpy as np
        NUM_EXPERTS = 8
        TOP_K = 2
        DIM = 128
        HIDDEN = 512
        B, S = (2, 128)
        key = jax.random.key(seed)
        k_x, k_g, k_1, k_2, k_3 = jax.random.split(key, 5)
        s_d = 1.0 / np.sqrt(DIM)
        s_h = 1.0 / np.sqrt(HIDDEN)
        return {'x': jax.random.normal(k_x, (B, S, DIM), dtype=jnp.float32), 'gate_w': jax.random.normal(k_g, (NUM_EXPERTS, DIM), dtype=jnp.float32) * s_d, 'w1': jax.random.normal(k_1, (NUM_EXPERTS, HIDDEN, DIM), dtype=jnp.float32) * s_d, 'w2': jax.random.normal(k_2, (NUM_EXPERTS, DIM, HIDDEN), dtype=jnp.float32) * s_h, 'w3': jax.random.normal(k_3, (NUM_EXPERTS, HIDDEN, DIM), dtype=jnp.float32) * s_d}
    _L0_ffn_all = _L0_ffn_setup()
    _L0_ffn_in = {k: v for k, v in _L0_ffn_all.items() if k in ('gate_w', 'w1', 'w2', 'w3')}
    del _L0_ffn_all
    return {'x': x, 'ctx_1024': ctx_1024, 'L0_xattn_Wq': _L0_xattn_in['Wq'], 'L0_xattn_bq': _L0_xattn_in['bq'], 'L0_xattn_Wk': _L0_xattn_in['Wk'], 'L0_xattn_bk': _L0_xattn_in['bk'], 'L0_xattn_Wv': _L0_xattn_in['Wv'], 'L0_xattn_bv': _L0_xattn_in['bv'], 'L0_xattn_Wo': _L0_xattn_in['Wo'], 'L0_attn_w_qkv': _L0_attn_in['w_qkv'], 'L0_attn_b_qkv': _L0_attn_in['b_qkv'], 'L0_attn_a_q': _L0_attn_in['a_q'], 'L0_attn_b_q': _L0_attn_in['b_q'], 'L0_attn_a_v': _L0_attn_in['a_v'], 'L0_attn_b_v': _L0_attn_in['b_v'], 'L0_attn_w_proj': _L0_attn_in['w_proj'], 'L0_attn_b_proj': _L0_attn_in['b_proj'], 'L0_ffn_gate_w': _L0_ffn_in['gate_w'], 'L0_ffn_w1': _L0_ffn_in['w1'], 'L0_ffn_w2': _L0_ffn_in['w2'], 'L0_ffn_w3': _L0_ffn_in['w3']}

def reference(x, ctx_1024, L0_xattn_Wq, L0_xattn_bq, L0_xattn_Wk, L0_xattn_bk, L0_xattn_Wv, L0_xattn_bv, L0_xattn_Wo, L0_attn_w_qkv, L0_attn_b_qkv, L0_attn_a_q, L0_attn_b_q, L0_attn_a_v, L0_attn_b_v, L0_attn_w_proj, L0_attn_b_proj, L0_ffn_gate_w, L0_ffn_w1, L0_ffn_w2, L0_ffn_w3):
    import jax
    import jax.numpy as jnp

    def _L0_xattn_ref(xq, xk, xv, Wq, bq, Wk, bk, Wv, bv, Wo):
        import jax, jax.numpy as jnp
        import numpy as np
        EMBED = 128
        HEADS = 16
        HEAD_DIM = EMBED // HEADS
        B, N, _ = xq.shape
        M = xk.shape[1]
        scale = HEAD_DIM ** (-0.5)
        q = (xq @ Wq.T + bq).reshape(B, N, HEADS, HEAD_DIM).transpose(0, 2, 1, 3)
        k = (xk @ Wk.T + bk).reshape(B, M, HEADS, HEAD_DIM).transpose(0, 2, 1, 3)
        v = (xv @ Wv.T + bv).reshape(B, M, HEADS, HEAD_DIM).transpose(0, 2, 1, 3)
        scores = jnp.einsum('bhnd,bhmd->bhnm', q, k) * scale
        weights = jax.nn.softmax(scores, axis=-1)
        out = jnp.einsum('bhnm,bhmd->bhnd', weights, v)
        out = out.transpose(0, 2, 1, 3).reshape(B, N, EMBED)
        return out @ Wo.T

    def _L0_attn_ref(x, w_qkv, b_qkv, a_q, b_q, a_v, b_v, w_proj, b_proj):
        import jax, jax.numpy as jnp
        import numpy as np
        B, N, C = (2, 256, 128)
        H = 16
        HD = C // H
        R = 16
        LORA_SCALE = 32.0 / R
        ATTN_SCALE = HD ** (-0.5)
        Bb, Nn, Cc = x.shape
        qkv = (x @ w_qkv + b_qkv).reshape(Bb, Nn, 3, H, HD).transpose(2, 0, 3, 1, 4)
        q, k, v = (qkv[0], qkv[1], qkv[2])
        q = q + jnp.einsum('bhnr,rd->bhnd', jnp.einsum('bhnd,dr->bhnr', q, a_q), b_q) * LORA_SCALE
        v = v + jnp.einsum('bhnr,rd->bhnd', jnp.einsum('bhnd,dr->bhnr', v, a_v), b_v) * LORA_SCALE
        attn = jax.nn.softmax(jnp.einsum('bhnd,bhmd->bhnm', q, k) * ATTN_SCALE, axis=-1)
        out = jnp.einsum('bhnm,bhmd->bhnd', attn, v)
        out = out.transpose(0, 2, 1, 3).reshape(Bb, Nn, Cc)
        return out @ w_proj + b_proj

    def _L0_ffn_ref(x, gate_w, w1, w2, w3):
        import jax, jax.numpy as jnp
        import numpy as np
        NUM_EXPERTS = 8
        TOP_K = 2
        DIM = 128
        HIDDEN = 512
        B, S = (2, 128)
        orig_shape = x.shape
        xt = x.reshape(-1, orig_shape[-1])
        scores = xt @ gate_w.T
        top_vals, top_idx = jax.lax.top_k(scores, TOP_K)
        top_w = jax.nn.softmax(top_vals, axis=-1)
        combine = jnp.einsum('tke,tk->te', jax.nn.one_hot(top_idx, NUM_EXPERTS, dtype=xt.dtype), top_w)
        h = jax.nn.silu(jnp.einsum('td,ehd->eth', xt, w1)) * jnp.einsum('td,ehd->eth', xt, w3)
        ye = jnp.einsum('eth,edh->etd', h, w2)
        y = jnp.einsum('te,etd->td', combine, ye)
        return y.reshape(orig_shape)
    x = x + _L0_xattn_ref(_layernorm(x, axis=-1), ctx_1024, ctx_1024, L0_xattn_Wq, L0_xattn_bq, L0_xattn_Wk, L0_xattn_bk, L0_xattn_Wv, L0_xattn_bv, L0_xattn_Wo)
    x = x + _L0_attn_ref(_layernorm(x, axis=-1), L0_attn_w_qkv, L0_attn_b_qkv, L0_attn_a_q, L0_attn_b_q, L0_attn_a_v, L0_attn_b_v, L0_attn_w_proj, L0_attn_b_proj)
    x = x + _L0_ffn_ref(_layernorm(x, axis=-1), L0_ffn_gate_w, L0_ffn_w1, L0_ffn_w2, L0_ffn_w3)
    return x

_drawn_inputs = setup_inputs


def setup_inputs(seed=0):
    import zlib

    import numpy as np

    out = dict(_drawn_inputs(seed))
    spreads = {'L0_xattn_bq': (0.0, 0.1), 'L0_xattn_bk': (0.0, 0.1), 'L0_xattn_bv': (0.0, 0.1)}
    factors = {}
    for name, (base, spread) in spreads.items():
        noise = np.random.default_rng([zlib.crc32(name.encode()), seed]).standard_normal(out[name].shape)
        drawn = base * np.exp(spread * noise) if base else spread * noise
        out[name] = jnp.asarray(drawn.astype(out[name].dtype))
    for name, factor in factors.items():
        out[name] = (out[name] * factor).astype(out[name].dtype)
    return out
```

```python
from contextlib import ExitStack

import concourse.bass as bass
from concourse import mybir
import numpy as np

F32 = mybir.dt.float32
BF16 = mybir.dt.bfloat16
U32 = mybir.dt.uint32
ALU = mybir.AluOpType
ACT = mybir.ActivationFunctionType
AX = mybir.AxisListType

B, N, C = 32, 64, 128
M = 1601
H, D = 16, 8
T = B * N
TILES = T // 128
PAIRS = H // 2
GROUPS = 2
GP = PAIRS // GROUPS
MT = -(-M // 128)
MPAD = MT * 128
BLOCKS = -(-MT // 2)
LAST_ROWS = M - 128 * (MT - 1)
K_PART = [0, 0, 0, 1, 1, 2]
Q_PART = [0, 1, 2, 0, 1, 0]
SLOTS = len(K_PART)
ROWS = SLOTS * 2 * D
CUTS = [(0, 402), (402, 400), (802, 400), (1202, 399)]
NCUT = len(CUTS)
UC = GP * NCUT
S1_AT = [3, 3, 3, 3, 3, 1, 0]
VT = 4
NV = -(-MT // VT)
EXPERTS, HID, TOPK = 8, 512, 2
HT = HID // 128
CHUNK = 512
CHUNKS = T // CHUNK
CT = CHUNK // 128
EPS = 1e-5
SCALE = float(D) ** -0.5
LORA = 2.0
R = 16
STACK_DMAS = SLOTS * GP
LN_STEPS = 4
SUM_ROWS = [16 + n % 16 for n in range(32)]
N_SW = 13
FIRST, LAST = 1, B // 2 - 2

INS = {
    "x": (T, C), "ctxT": (B, C, M), "WqT": (C, C), "WkT": (C, C), "WvT": (C, C), "WoP": (128, GROUPS, 2, C),
    "bq": (C, 1), "bk": (C, 1), "bv": (1, C), "wqT": (C, C), "wk": (C, C), "wvT": (C, C),
    "sbq": (C, 1), "sbk": (C, 1), "sbv": (C, 128), "aqT": (R, C), "bbq": (R, C), "avT": (R, C), "bbv": (R, C),
    "WpP": (128, GROUPS, 2, C), "bp": (1, C), "gateT": (C, EXPERTS), "W1T": (C, EXPERTS, HID),
    "W3T": (C, EXPERTS, HID), "W2T": (128, EXPERTS, HT, C),
    "ident": (128, 128), "head_rows": (128, 2), "head_block": (128, 128), "iota": (128, EXPERTS),
}


class Batch:

    def __init__(self, i, off):
        self.i, self.off = i, off

    def __add__(self, k):
        return Batch(self.i, self.off + k)

    def __sub__(self, k):
        return Batch(self.i, self.off - k)


def parity(b):
    return (b if isinstance(b, int) else b.off) % 2


def value(b):
    return b if isinstance(b, int) else b.i * 2 + b.off


def count(f, b):
    if isinstance(b, int):
        return f(b)
    slope = f(b.off + 2 * FIRST + 2) - f(b.off + 2 * FIRST)
    return b.i * slope + (f(b.off + 2 * FIRST) - slope * FIRST)


def uses():
    out = [("k", b, c) for b in (0, 1) for c in range(NCUT)] + [("v", 0, c) for c in range(NV)] + [("m", 0, 0)]
    for b in range(B):
        out.append(("m", b, 1))
        if b:
            out.append(("y", b - 1, 0))
        for c in range(NCUT):
            out += [("k", b + 2, c)] * (b + 2 < B) + [("v", b + 1, c)] * (b + 1 < B)
        out += [("m", b + 1, 0)] * (b + 1 < B)
    out.append(("y", B - 1, 0))
    return out


ORDER = uses()
USE = {u: n for n, u in enumerate(ORDER)}


def perceiver(nc, t, out):
    ctx = ExitStack()
    scope = ExitStack()

    def sb(name, shape, dt=F32, where=ctx):
        return where.enter_context(nc.sbuf_tensor(name, shape, dt))

    def sem(name):
        return ctx.enter_context(nc.semaphore(name))

    def wait(eng, s, v):
        if not isinstance(v, int) or v > 0:
            eng.wait_ge(s, v)

    with ctx:
        x_all = sb("x_all", [128, TILES, C])
        ident = sb("ident_sb", [128, 128])
        identb = sb("identb", [128, 128], BF16)
        head_rows = sb("head_rows_sb", [128, 2])
        eps = sb("eps", [128, 1])
        stats = sb("stats", [128, TILES, 6])
        mv = sb("mv", [128, TILES, 2])
        std = sb("std", [128, TILES])
        rstd = sb("rstd", [128, TILES])
        biases = sb("biases", [128, 8])
        BQ, BK, SBQ, SBK, SBV, SBQ2 = (biases[:, n:n + 1] for n in range(6))
        WqT, WkT, WvT = (sb(n, [128, 128]) for n in ("WqT_sb", "WkT_sb", "WvT_sb"))
        WoP = sb("WoP_sb", [128, GROUPS, 2, C])
        bv4 = sb("bv4", [128, VT, C])
        Qall = sb("Qall", [128, PAIRS, T], BF16)

        Kst = sb("Kst", [128, 2, PAIRS, MPAD], BF16, scope)
        Kpart = sb("Kpart", [128, 2, 3, M], BF16, scope)
        Krest = sb("Krest", [128, 2, CUTS[0][1]], F32, scope)
        V = sb("V", [128, 2, MT, PAIRS, 32], F32, scope)
        P = sb("P", [128, BLOCKS, 1024], F32, scope)
        ctxT = sb("ctxT_sb", [128, 2, M], F32, scope)
        Qst = sb("Qst", [128, 2, GP, 128], BF16, scope)
        mxc = sb("mxc", [128, 2, GP, NCUT], F32, scope)
        nmf = sb("nmf", [128, 2, GP], F32, scope)
        nmp = sb("nmp", [128, 2, GP, 3], BF16, scope)
        den = sb("den", [128, 2, 128], F32, scope)
        O = sb("O", [128, 2, 128], F32, scope)
        rden = sb("rden", [128, 2, 128], F32, scope)
        On = sb("On", [128, 2, 128], F32, scope)
        xnT0 = P[:, 0:2, :].rearrange("p a b -> p (a b)")
        qf0 = P[:, 2:4, :].rearrange("p a b -> p (a b)")
        qparts0 = P[:, 4:7, :].rearrange("p a b -> p (a b)").bitcast(BF16).rearrange("p (k t) -> p k t", k=3)
        xn0 = V[:, 0, 0:8, :, :].rearrange("p a b c -> p (a b c)").rearrange("p (t c) -> p t c", c=C)
        scope.close()

        W1T = sb("W1T_sb", [128, EXPERTS, HID])
        W3T = sb("W3T_sb", [128, EXPERTS, HID])
        W2T = sb("W2T_sb", [128, EXPERTS, HT, C])
        gateT = sb("gateT_sb", [128, EXPERTS])
        iota = sb("iota_sb", [128, EXPERTS])
        xn1 = sb("xn1", [128, TILES, C])
        xnT1 = sb("xnT1", [128, T])
        scope2 = ExitStack()
        Kall = sb("Kall", [128, PAIRS, T], BF16, scope2)
        qf1 = sb("qf1", [128, T], F32, scope2)
        qparts1 = sb("qparts1", [128, 3, T], BF16, scope2)
        V2 = sb("V2", [128, TILES, C], F32, scope2)
        V2st = sb("V2st", [128, 2, PAIRS, 32], F32, scope2)
        P2 = sb("P2", [128, PAIRS, 128], F32, scope2)
        K2st = sb("K2st", [128, 2, PAIRS, 128], BF16, scope2)
        Q2st = sb("Q2st", [128, 2, 2, PAIRS, 128], BF16, scope2)
        lw = sb("lw", [128, 10, 128], F32, scope2)
        lora = sb("lora", [R, 4, C], F32, scope2)
        sbvc = sb("sbvc", [128, 128], F32, scope2)
        bv2 = sb("bv2", [128, C], F32, scope2)
        bp = sb("bp_sb", [128, C], F32, scope2)
        WpP = sb("WpP_sb", [128, GROUPS, 2, C], F32, scope2)
        nmf2 = sb("nmf2", [128, 2, 16], F32, scope2)
        nmp2 = sb("nmp2", [128, 2, 16, 3], BF16, scope2)
        den2 = sb("den2", [128, 4, 128], F32, scope2)
        rden2 = sb("rden2", [128, 4, 128], F32, scope2)
        On2 = sb("On2", [128, 4, 128], F32, scope2)
        ytmp = sb("ytmp", [128, C], F32, scope2)
        scope2.close()
        gs = sb("gs", [128, TILES, 8])
        top = sb("top", [128, TILES, 8])
        topi = sb("topi", [128, TILES, 8], U32)
        topf = sb("topf", [128, TILES, 8])
        tw = sb("tw", [128, 4, TILES])
        comb = sb("comb", [128, TILES, EXPERTS])
        comb2 = sb("comb2", [128, TILES, EXPERTS])
        sil = sb("sil", [128, 2, CHUNK])
        hT = sb("hT", [128, 2, HT, CHUNK])
        acc = sb("acc", [128, 2, CT, C])
        out_t = sb("out_t", [128, 2, CT, C])

        ps = ctx.enter_context(nc.psum_tensor("ps", [128, 8, 512], F32))
        psS1 = ps[:, 0:2, :]
        psS2 = ps[:, 2:6, :].rearrange("p (n k) c -> p n (k c)", n=2)
        psO = ps[:, 6, :]
        psM = ps[:, 7, :]

        load = sem("load")
        w_in = sem("w_in")
        sw_in = sem("sw_in")
        fw_in = sem("fw_in")
        made = sem("made")
        pads = sem("pads")
        ctx_in = [sem(f"ctx_in{n}") for n in range(2)]
        kst_in = [[sem(f"kst_in{n}{g}") for g in range(GROUPS)] for n in range(2)]
        qst_in = sem("qst_in")
        s1_done = sem("s1_done")
        s2_done = sem("s2_done")
        av_done = sem("av_done")
        bank_full = sem("bank_full")
        exp_done = sem("exp_done")
        khi_done = sem("khi_done")
        max_rows = sem("max_rows")
        max_done = sem("max_done")
        nm_chain = sem("nm_chain")
        o_read = sem("o_read")
        norm_chain = sem("norm_chain")
        norm_done = sem("norm_done")
        qst_done = sem("qst_done")
        krest_done = sem("krest_done")
        kmid_done = sem("kmid_done")
        klo_done = sem("klo_done")
        v_done = sem("v_done")
        x1_done = sem("x1_done")
        ln_stat = sem("ln_stat")
        ln_std = sem("ln_std")
        ln_tr = sem("ln_tr")
        ln_ev = sem("ln_ev")
        proj = sem("proj")
        proj_ev = sem("proj_ev")
        split = sem("split")
        stack_in = sem("stack_in")
        lora_pe = sem("lora_pe")
        lora_ev = sem("lora_ev")
        b_st = sem("b_st")
        b_s1 = sem("b_s1")
        b_chain = sem("b_chain")
        b_nm = sem("b_nm")
        b_rows = sem("b_rows")
        b_s2 = sem("b_s2")
        b_exp = sem("b_exp")
        b_v = sem("b_v")
        b_av = sem("b_av")
        b_norm = sem("b_norm")
        b_y = sem("b_y")
        vals = sem("vals")
        b_xa = sem("b_xa")
        b_x = sem("b_x")
        g_pe = sem("g_pe")
        g_chain = sem("g_chain")
        g_exp = sem("g_exp")
        h_pe = sem("h_pe")
        h_sil = sem("h_sil")
        h_done = sem("h_done")
        y_pe = sem("y_pe")
        y_done = sem("y_done")
        o_done = sem("o_done")
        o_out = [sem(f"o_out{n}") for n in range(2)]

        def wait_alone(eng, s, v):
            v = v if isinstance(v, int) else eng.snap(eng.to_reg(v))
            eng.wait_ge(load, 16)
            wait(eng, s, v)

        N_LOAD, N_W = 4, 3 + 2 + VT
        block = ctx.enter_context(nc.Block())

        def over_batches(eng, body):
            for b in range(2 * FIRST):
                body(b)
            with eng.Fori(FIRST, LAST + 1) as i:
                for off in range(2):
                    body(Batch(i, off))
            for b in range(2 * LAST + 2, B):
                body(b)

        def there(b, lo, hi):
            return lo <= b < hi if isinstance(b, int) else True

        def units(b, g):
            return lambda k, add: count(lambda n: k * (2 * n + g) + add, b)

        def neighbour(b, g, k):
            n = g + k
            return b + n // 2, n % 2

        @block.sync
        def _(sp):
            sp.dma_start(x_all[:], t["x"].rearrange("(n p) c -> p n c", p=128)).then_inc(load, 16)
            sp.dma_start(ident[:], t["ident"]).then_inc(load, 16)
            sp.dma_start(head_rows[:], t["head_rows"]).then_inc(load, 16)
            sp.dma_start(BQ, t["bq"]).then_inc(load, 16)
            sp.dma_start(WqT[:], t["WqT"]).then_inc(w_in, 16)
            sp.dma_start(WkT[:], t["WkT"]).then_inc(w_in, 16)
            sp.dma_start(BK, t["bk"]).then_inc(w_in, 16)
            sp.dma_start(ctxT[:, 0, :], t["ctxT"][0]).then_inc(ctx_in[0], 16)
            sp.dma_start(ctxT[:, 1, :], t["ctxT"][1]).then_inc(ctx_in[1], 16)
            sp.dma_start(WvT[:], t["WvT"]).then_inc(w_in, 16)
            sp.dma_start(WoP[:], t["WoP"]).then_inc(w_in, 16)
            for n in range(VT):
                sp.dma_start(bv4[:, n, :], t["bv"].to_broadcast((128, C))).then_inc(w_in, 16)
            for part in range(3):
                sp.wait_ge(split, [1, 3, 4][part])
                for s in range(SLOTS):
                    if Q_PART[s] == part:
                        for p in range(PAIRS):
                            sp.dma_start(Qall[16 * s:16 * s + 16, p, :],
                                         qparts0[16 * p:16 * p + 16, part, :]).then_inc(qst_in, 16)

            def stack(b):
                wait_alone(sp, klo_done, count(lambda n: NCUT * (n + 1), b))
                for g in range(GROUPS):
                    if there(b, 2, B):
                        wait_alone(sp, s2_done, count(lambda n: BLOCKS * (2 * (n - 2) + g + 1), b))
                    for s in range(SLOTS):
                        for p in range(GP * g, GP * g + GP):
                            sp.dma_start(Kst[16 * s:16 * s + 16, parity(b), p, 0:M],
                                         Kpart[16 * p:16 * p + 16, parity(b), K_PART[s], :])\
                              .then_inc(kst_in[parity(b)][g], 16)

            stack(0)

            def batch(b):
                if there(b, 0, B - 1):
                    stack(b + 1)
                if there(b, 0, B - 2):
                    wait_alone(sp, bank_full, count(lambda n: 1 + USE["v", n, NV - 1], b))
                    sp.dma_start(ctxT[:, parity(b), :],
                                 t["ctxT"][bass.ds(value(b + 2), 1)].rearrange("o c m -> (o c) m"))\
                      .then_inc(ctx_in[parity(b)], 16)

            over_batches(sp, batch)

            sp.wait_ge(x1_done, B)
            for n, name in enumerate(("wqT", "wk", "wvT")):
                sp.dma_start(lw[:, n, :], t[name]).then_inc(sw_in, 16)
            sp.dma_start(lw[:, 7, :], t["head_block"]).then_inc(sw_in, 16)
            for n, name in enumerate(("aqT", "bbq", "avT", "bbv")):
                sp.dma_start(lora[:, n, :], t[name]).then_inc(sw_in, 16)
            sp.dma_start(SBQ, t["sbq"]).then_inc(sw_in, 16)
            sp.dma_start(SBK, t["sbk"]).then_inc(sw_in, 16)
            sp.dma_start(sbvc[:], t["sbv"]).then_inc(sw_in, 16)
            sp.dma_start(WpP[:], t["WpP"]).then_inc(sw_in, 16)
            sp.dma_start(bp[:], t["bp"].to_broadcast((128, C))).then_inc(sw_in, 16)
            for name, dst in (("gateT", gateT), ("iota", iota), ("W1T", W1T), ("W3T", W3T), ("W2T", W2T)):
                sp.dma_start(dst[:], t[name]).then_inc(fw_in, 16)
            for part in range(3):
                sp.wait_ge(split, 4 + [1, 3, 4][part])
                for s in range(SLOTS):
                    if Q_PART[s] == part:
                        for p in range(PAIRS):
                            sp.dma_start(Qall[16 * s:16 * s + 16, p, :],
                                         qparts1[16 * p:16 * p + 16, part, :]).then_inc(stack_in, 16)
            for part in range(3):
                sp.wait_ge(split, 8 + [1, 3, 4][part])
                for s in range(SLOTS):
                    if K_PART[s] == part:
                        for p in range(PAIRS):
                            sp.dma_start(Kall[16 * s:16 * s + 16, p, :],
                                         qparts1[16 * p:16 * p + 16, part, :]).then_inc(stack_in, 16)
            with sp.Fori(0, CHUNKS // 2) as i:
                for k in range(2):
                    wait_alone(sp, o_done, i * 2 + k + 1)
                    sp.dma_start(out[bass.ds(i * (2 * CHUNK) + k * CHUNK, CHUNK), :].rearrange("(n p) c -> p n c", p=128),
                                 out_t[:, k]).then_inc(o_out[k], 16)
            for k in range(2):
                sp.wait_ge(o_out[k], 16 * (CHUNKS // 2))

        @block.gpsimd
        def _(pool):
            for n in range(2):
                nc.gpsimd.memset(Kst[96:99, n, :, :], 1.0).then_inc(pads, 1)
                pool.wait_ge(pads, 2 * n + 1)
                nc.gpsimd.memset(Kst[0:96, n, :, M:MPAD], 0.0).then_inc(pads, 1)
                pool.wait_ge(pads, 2 * n + 2)
            pool.wait_ge(ln_tr, TILES // 4)
            for n in range(2):
                nc.gpsimd.memset(V[:, n, :, :, 16:32], 1.0).then_inc(pads, 1)
                pool.wait_ge(pads, n + 5)

            def low_part(b):
                for c, (at, w) in enumerate(CUTS):
                    pool.wait_ge(kmid_done, count(lambda n: NCUT * n + c + 1, b))
                    nc.gpsimd.tensor_tensor(Kpart[:, parity(b), 2, at:at + w], Krest[:, c % 2, 0:w],
                                            Kpart[:, parity(b), 1, at:at + w], ALU.subtract).then_inc(klo_done, 1)
                    pool.wait_ge(klo_done, count(lambda n: NCUT * n + c + 1, b))

            over_batches(pool, low_part)
            pool.wait_ge(x1_done, B)
            nc.gpsimd.memset(V2st[:, :, :, 16:32], 1.0).then_inc(pads, 1)
            for n in range(2):
                pool.wait_ge(pads, n + 7)
                nc.gpsimd.memset(K2st[96:99, n, :, :], 1.0).then_inc(pads, 1)

        @block.tensor
        def _(pe):
            mm = nc.tensor.matmul

            def turn_tiles(k, xn):
                pe.wait_ge(ln_stat, LN_STEPS * (k + 1))
                for q in range(TILES // 4):
                    n = k * (TILES // 4) + q
                    for j in range(4):
                        last = nc.tensor.transpose(ps[:, q % 4, 128 * j:128 * j + 128], xn[:, 4 * q + j, :], ident[:])
                    last.then_inc(ln_tr, 1)

            turn_tiles(0, xn0)
            pe.wait_ge(w_in, 16 * N_W)
            for q in range(4):
                pe.wait_ge(ln_ev, q + 1)
                mm(ps[:, 4 + q, :], WqT[:], xnT0[:, 512 * q:512 * q + 512], start=True, stop=True).then_inc(proj, 1)

            def bank(kind, b, c):
                some = b if isinstance(b, int) else b.off + 2 * FIRST
                if USE[kind, some, c] == 0:
                    return
                last, bb, cc = ORDER[USE[kind, some, c] - 1]
                read, of_batch = {"k": (krest_done, NCUT), "v": (v_done, NV), "m": (max_rows, GROUPS),
                                  "y": (x1_done, 1)}[last]
                pe.wait_ge(read, count(lambda n: of_batch * (n + bb - some) + cc + 1, b))

            def k_chunk(b, c):
                at, w = CUTS[c]
                bank("k", b, c)
                if c == 0:
                    pe.wait_ge(ctx_in[parity(b)], count(lambda n: 16 * (n // 2 + 1), b))
                mm(psM[:, 0:w], WkT[:], ctxT[:, parity(b), at:at + w], start=True, stop=True).then_inc(bank_full, 1)

            def v_chunk(b, c):
                bank("v", b, c)
                for m in range(VT * c, min(VT * c + VT, MT)):
                    w = 128 if m < MT - 1 else LAST_ROWS
                    last = mm(psM[0:w, 128 * (m - VT * c):128 * (m - VT * c) + 128],
                              ctxT[:, parity(b), 128 * m:128 * m + w], WvT[:], start=True, stop=True)
                last.then_inc(bank_full, 1)

            def s1(b, g, n):
                u = units(b, g)
                j, c = divmod(n, NCUT)
                at, w = CUTS[c]
                if n == 0:
                    pe.wait_ge(qst_done, u(1, 1))
                    pe.wait_ge(kst_in[parity(b)][g], count(lambda k: 16 * STACK_DMAS * (k // 2 + 1), b))
                wait(pe, max_done, u(UC, n - 1))
                mm(psS1[:, n % 2, 0:w], Qst[0:ROWS, g, j, :], Kst[0:ROWS, parity(b), GP * g + j, at:at + w],
                   start=True, stop=True).then_inc(s1_done, 1)

            def max_to_rows(b, g):
                bank("m", b, g)
                pe.wait_ge(nm_chain, units(b, g)(5, 5))
                for j in range(GP):
                    last = mm(psM[96:99, 128 * j:128 * j + 128], nmp[:, g, j, :], identb[:], start=True, stop=True)
                last.then_inc(bank_full, 1)

            def s2(b, g, s):
                u = units(b, g)
                if s == 0:
                    pe.wait_ge(max_rows, u(1, 1))
                wait(pe, exp_done, u(BLOCKS, s - 1))
                for m in range(2 * s, min(2 * s + 2, MT)):
                    for j in range(GP):
                        o = 512 * (m % 2) + 128 * j
                        last = mm(psS2[:, (BLOCKS * g + s) % 2, o:o + 128],
                                  Kst[0:ROWS + 3, parity(b), GP * g + j, 128 * m:128 * m + 128],
                                  Qst[0:ROWS + 3, g, j, :], start=True, stop=True)
                last.then_inc(s2_done, 1)

            def av(b, g, s):
                u = units(b, g)
                if s == 0:
                    pe.wait_ge(v_done, count(lambda n: NV * (n + 1), b))
                    wait(pe, o_read, u(1, 0))
                pe.wait_ge(exp_done, u(BLOCKS, s + 1))
                for m in range(2 * s, min(2 * s + 2, MT)):
                    w = 128 if m < MT - 1 else LAST_ROWS
                    for j in range(GP):
                        o = 512 * (m % 2) + 128 * j
                        last = mm(psO[32 * j:32 * j + 32, 0:128], V[0:w, parity(b), m, GP * g + j, :],
                                  P[0:w, s, o:o + 128], start=(m == 0), stop=(m == MT - 1))
                last.then_inc(av_done, 1)

            def project_out(b):
                bank("y", b, 0)
                pe.wait_ge(norm_done, units(b, 1)(1, 1))
                r = N * parity(b)
                for g in range(GROUPS):
                    for h in range(2):
                        last = mm(psM[r:r + N, 0:C], On[:, g, N * h:N * h + N], WoP[:, g, h, :],
                                  start=(g == 0 and h == 0), stop=(g == 1 and h == 1))
                last.then_inc(bank_full, 1)

            pe.wait_ge(pads, 6)
            pe.wait_ge(made, 1)
            pe.wait_ge(proj_ev, 4)
            for b in range(2):
                for c in range(NCUT):
                    k_chunk(b, c)
            for c in range(NV):
                v_chunk(0, c)
            for n in range(UC):
                s1(0, 0, n)
            max_to_rows(0, 0)

            def step(b, g):
                prev, nxt = neighbour(b, g, -1), neighbour(b, g, 1)
                n = 0
                for s in range(BLOCKS):
                    s2(b, g, s)
                    if s and there(prev[0], 0, B):
                        av(*prev, s)
                    if g == 1 and s == 1 and there(b, 1, B):
                        project_out(b - 1)
                    for k in range(S1_AT[s]):
                        if there(nxt[0], 0, B):
                            s1(*nxt, n)
                        n += 1
                        if g == 1 and 1 <= s <= NCUT:
                            if k == 0 and there(b, 0, B - 2):
                                k_chunk(b + 2, s - 1)
                            if k == 1 and there(b, 0, B - 1):
                                v_chunk(b + 1, s - 1)
                    if s == 0 and there(prev[0], 0, B):
                        av(*prev, s)
                    if s == BLOCKS - 1 and there(nxt[0], 0, B):
                        max_to_rows(*nxt)

            def batch(b):
                for g in range(GROUPS):
                    step(b, g)

            over_batches(pe, batch)
            for s in range(BLOCKS):
                av(B - 1, 1, s)
            project_out(B - 1)

            pe.wait_ge(sw_in, 16 * N_SW)
            mm(ps[:, 4, 0:128], lora[:, 0, :], lora[:, 1, :], start=True, stop=True)
            mm(ps[:, 5, 0:128], lora[:, 2, :], lora[:, 3, :], start=True, stop=True).then_inc(lora_pe, 1)
            pe.wait_ge(lora_ev, 4)
            mm(ps[:, 6, 0:128], lw[:, 0, :], lw[:, 5, :], start=True, stop=True)
            mm(ps[:, 6, 128:256], lw[:, 2, :], lw[:, 6, :], start=True, stop=True)
            mm(ps[:, 6, 256:384], sbvc[:], lw[:, 6, :], start=True, stop=True)
            mm(ps[:, 6, 384:386], lw[:, 5, :], biases[:, 2:4], start=True, stop=True).then_inc(lora_pe, 1)
            turn_tiles(1, xn1)
            pe.wait_ge(lora_ev, 8)
            for w in range(2):
                for q in range(4):
                    pe.wait_ge(ln_ev, 4 + q + 1)
                    n = 4 + 4 * w + q
                    if w:
                        pe.wait_ge(proj_ev, n - 3)
                    mm(ps[:, 4 + q, :], lw[:, 3 if w == 0 else 1, :], xnT1[:, 512 * q:512 * q + 512],
                       start=True, stop=True).then_inc(proj, 1)
            for q in range(4):
                for j in range(4):
                    m = 4 * q + j
                    last = mm(ps[:, q, 128 * j:128 * j + 128], xnT1[:, 128 * m:128 * m + 128], lw[:, 4, :],
                              start=True, stop=True)
                last.then_inc(proj, 1)
            pe.wait_ge(pads, 9)

            def scores_for_max(j):
                pe.wait_ge(b_st, j + 1)
                wait(pe, b_rows, 2 * j if isinstance(j, int) else j * 2)
                for e in range(2):
                    for p in range(PAIRS):
                        last = mm(ps[:, e, N * p:N * p + N], Q2st[0:ROWS, JP(j), e, p, :],
                                  K2st[0:ROWS, JP(j), p, N * e:N * e + N], start=True, stop=True)
                last.then_inc(b_s1, 1)

            def rows_of_max(j):
                pe.wait_ge(b_chain, j * 5 + 5)
                if not isinstance(j, int) or j > 1:
                    pe.wait_ge(b_x, j - 1)
                for e in range(2):
                    for p in range(PAIRS):
                        last = mm(ps[96:99, 2 * e + p // 4, 128 * (p % 4):128 * (p % 4) + 128],
                                  nmp2[:, JP(j), PAIRS * e + p, :], identb[:], start=True, stop=True)
                    last.then_inc(b_nm, 1)

            def JP(j):
                return j % 2 if isinstance(j, int) else JPAR[0]

            JPAR = [0]

            def shifted_scores(j):
                pe.wait_ge(b_rows, j * 2 + 2)
                wait(pe, b_exp, j)
                for e in range(2):
                    for p in range(PAIRS):
                        last = mm(ps[N * e:N * e + N, 4 + p // 4, 128 * (p % 4):128 * (p % 4) + 128],
                                  K2st[0:ROWS + 3, JP(j), p, N * e:N * e + N], Q2st[0:ROWS + 3, JP(j), e, p, :],
                                  start=True, stop=True)
                last.then_inc(b_s2, 1)

            def values(j):
                pe.wait_ge(b_exp, j + 1)
                pe.wait_ge(b_v, j + 1)
                wait_alone(pe, b_norm, j * 3)
                for e in range(2):
                    for p in range(PAIRS):
                        q = 32 * (p % 4)
                        last = mm(ps[q:q + 32, 6 + e, 128 * (p // 4):128 * (p // 4) + 128],
                                  V2st[N * e:N * e + N, JP(j), p, :], P2[N * e:N * e + N, p, :], start=True, stop=True)
                last.then_inc(b_av, 1)

            def outputs(j, more):
                pe.wait_ge(b_norm, j * 3 + 3)
                pe.wait_ge(b_rows, (j + 2) * 2 if more else 2 * TILES)
                for e in range(2):
                    for g in range(GROUPS):
                        for h in range(2):
                            last = mm(ps[N * e:N * e + N, 2, 0:C], On2[:, 2 * e + g, N * h:N * h + N], WpP[:, g, h, :],
                                      start=(g == 0 and h == 0), stop=(g == 1 and h == 1))
                last.then_inc(b_y, 1)

            pe.wait_ge(vals, 4)
            pe.wait_ge(proj_ev, 12)
            pe.wait_ge(stack_in, 16 * 2 * SLOTS * PAIRS)
            scores_for_max(0)
            rows_of_max(0)

            def pair(j, par, more=True):
                JPAR[0] = (par + 1) % 2
                if more:
                    scores_for_max(j + 1)
                JPAR[0] = par
                shifted_scores(j)
                JPAR[0] = (par + 1) % 2
                if more:
                    rows_of_max(j + 1)
                JPAR[0] = par
                values(j)
                outputs(j, more)

            pair(0, 0)
            with pe.Fori(0, (TILES - 2) // 2) as i:
                pair(i * 2 + 1, 1)
                pair(i * 2 + 2, 0)
            pair(TILES - 1, 1, more=False)

            turn_tiles(2, xn1)
            pe.wait_ge(ln_ev, 12)
            pe.wait_ge(fw_in, 16 * 5)
            for m in range(TILES):
                last = mm(ps[:, 4, 8 * m:8 * m + 8], xnT1[:, 128 * m:128 * m + 128], gateT[:], start=True, stop=True)
            last.then_inc(g_pe, 1)
            pe.wait_ge(g_chain, 1)

            def hidden(q, e, m):
                n = q * (EXPERTS * HT) + (HT * e + m)
                if not isinstance(n, int) or n >= 2:
                    pe.wait_ge(h_done, n - 1)
                x_q = xnT1[:, bass.ds(q * CHUNK, CHUNK)]
                mm(ps[:, m % 2, :], W1T[:, e, 128 * m:128 * m + 128], x_q, start=True, stop=True)
                mm(ps[:, 2 + m % 2, :], W3T[:, e, 128 * m:128 * m + 128], x_q, start=True, stop=True).then_inc(h_pe, 1)

            def expert_out(q, e):
                n = q * EXPERTS + e
                pe.wait_ge(h_done, n * HT + HT)
                if not isinstance(n, int) or n >= 2:
                    pe.wait_ge(y_done, n - 1)
                for k in range(CT):
                    for m in range(HT):
                        last = mm(ps[:, 5 + e % 2, 128 * k:128 * k + 128], hT[:, e % 2, m, 128 * k:128 * k + 128],
                                  W2T[:, e, m, :], start=(m == 0), stop=(m == HT - 1))
                last.then_inc(y_pe, 1)

            def chunk(q, before):
                for e in range(EXPERTS):
                    for m in range(HT):
                        hidden(q, e, m)
                        if m == 1:
                            if e:
                                expert_out(q, e - 1)
                            elif before is not None:
                                expert_out(before, EXPERTS - 1)

            chunk(0, None)
            with pe.Fori(1, CHUNKS) as q:
                chunk(q, q - 1)
            expert_out(CHUNKS - 1, EXPERTS - 1)

        @block.scalar
        def _(act):
            def deviations(k):
                act.wait_ge(ln_stat, LN_STEPS * k + 2)
                nc.scalar.activation(std[:], mv[:, :, 1], ACT.Sqrt, bias=eps[:, 0:1]).then_inc(ln_std, 1)

            def evacuate(k, xnT):
                for q in range(TILES // 4):
                    act.wait_ge(ln_tr, k * (TILES // 4) + q + 1)
                    nc.scalar.activation(xnT[:, 512 * q:512 * q + 512], ps[:, q, :], ACT.Copy).then_inc(ln_ev, 1)

            deviations(0)
            evacuate(0, xnT0)

            def k_high(b, c):
                at, w = CUTS[c]
                if c == 0 and there(b, 2, B):
                    for g in range(GROUPS):
                        act.wait_ge(kst_in[parity(b)][g], count(lambda n: 16 * STACK_DMAS * (n // 2), b))
                act.wait_ge(bank_full, count(lambda n: USE["k", n, c] + 1, b))
                nc.scalar.activation(Kpart[:, parity(b), 0, at:at + w], psM[:, 0:w], ACT.Identity,
                                     bias=BK).then_inc(khi_done, 1)

            def exp(b, g, s):
                u = units(b, g)
                w = 1024 if s < BLOCKS - 1 or MT % 2 == 0 else 512
                act.wait_ge(s2_done, u(BLOCKS, s + 1))
                wait(act, av_done, u(BLOCKS, s + 1 - BLOCKS))
                nc.scalar.activation(P[:, s, 0:w], psS2[:, (BLOCKS * g + s) % 2, 0:w], ACT.Exp).then_inc(exp_done, 1)

            def rows(b, g):
                act.wait_ge(bank_full, count(lambda n: USE["m", n, g] + 1, b))
                act.wait_ge(qst_done, units(b, g)(1, 1))
                nc.scalar.activation(Qst[96:99, g, :, :], psM[96:99, :].rearrange("p (j q) -> p j q", j=GP),
                                     ACT.Copy).then_inc(max_rows, 1)

            act.wait_ge(w_in, 16 * N_W)
            for b in range(2):
                for c in range(NCUT):
                    k_high(b, c)
            rows(0, 0)
            act.wait_ge(qst_in, 16 * SLOTS * PAIRS)

            def batch(b):
                for g in range(GROUPS):
                    for s in range(BLOCKS):
                        exp(b, g, s)
                        if g == 1 and 1 <= s <= NCUT and there(b, 0, B - 2):
                            k_high(b + 2, s - 1)
                    nxt = neighbour(b, g, 1)
                    if there(nxt[0], 0, B):
                        rows(*nxt)

            over_batches(act, batch)

            deviations(1)
            evacuate(1, xnT1)

            def rows_in(j, par):
                for e in range(2):
                    act.wait_ge(b_nm, j * 2 + e + 1)
                    act.wait_ge(b_st, j + 1)
                    nc.scalar.activation(Q2st[96:99, par, e, :, :],
                                         ps[96:99, 2 * e:2 * e + 2, :].rearrange("p a (b q) -> p (a b) q", b=4),
                                         ACT.Copy).then_inc(b_rows, 1)

            def pair(j, par, more=True):
                if isinstance(j, int) and j < 2:
                    pass
                else:
                    act.wait_ge(b_av, j - 1)
                v = V2[:, j, :] if isinstance(j, int) else V2[:, bass.ds(j, 1), :].rearrange("p o c -> p (o c)")
                nc.scalar.activation(V2st[:, par, :, 0:16], v.rearrange("p (a b) -> p a b", b=16),
                                     ACT.Copy).then_inc(b_v, 1)
                act.wait_ge(b_s2, j + 1)
                wait(act, b_av, j)
                nc.scalar.activation(P2[:].rearrange("p a b -> p (a b)"),
                                     ps[:, 4:6, :].rearrange("p a b -> p (a b)"), ACT.Exp).then_inc(b_exp, 1)
                if more:
                    rows_in(j + 1, 1 - par)

            act.wait_ge(vals, 4)
            act.wait_ge(pads, 9)
            rows_in(0, 0)
            pair(0, 0)
            with act.Fori(0, (TILES - 2) // 2) as i:
                pair(i * 2 + 1, 1)
                pair(i * 2 + 2, 0)
            pair(TILES - 1, 1, more=False)

            deviations(2)
            evacuate(2, xnT1)
            act.wait_ge(g_chain, 4)
            nc.scalar.activation(tw[:, 1, :], tw[:, 0, :], ACT.Exp).then_inc(g_exp, 1)

            def silu(q, e, m):
                n = q * (EXPERTS * HT) + (HT * e + m)
                act.wait_ge(h_pe, n + 1)
                if not isinstance(n, int) or n >= 2:
                    act.wait_ge(h_done, n - 1)
                nc.scalar.activation(sil[:, m % 2, :], ps[:, m % 2, :], ACT.Silu).then_inc(h_sil, 1)

            def chunk(q):
                for e in range(EXPERTS):
                    for m in range(HT):
                        silu(q, e, m)

            chunk(0)
            with act.Fori(1, CHUNKS) as q:
                chunk(q)

        @block.vector
        def _(dve):
            v = nc.vector
            v.memset(eps[:], EPS)
            dve.wait_ge(load, 16 * N_LOAD)
            v.tensor_copy(identb[:], ident[:]).then_inc(made, 1)

            def normalise(k, xn):
                s0 = LN_STEPS * k
                for m in range(TILES):
                    last = v.bn_stats(stats[:, m, :], x_all[:, m, :])
                last.then_inc(ln_stat, 1)
                dve.wait_ge(ln_stat, s0 + 1)
                for m in range(TILES):
                    last = v.bn_aggr(mv[:, m, :], stats[:, m, :])
                last.then_inc(ln_stat, 1)
                dve.wait_ge(ln_std, k + 1)
                v.reciprocal(rstd[:], std[:]).then_inc(ln_stat, 1)
                dve.wait_ge(ln_stat, s0 + 3)
                for m in range(TILES):
                    last = v.tensor_scalar(xn[:, m, :], x_all[:, m, :], mv[:, m, 0:1], rstd[:, m:m + 1],
                                           ALU.subtract, ALU.mult)
                last.then_inc(ln_stat, 1)

            def project_and_split(n0, s0, bias, scale, qf, parts):
                for q in range(4):
                    dve.wait_ge(proj, n0 + q + 1)
                    v.tensor_scalar(qf[:, 512 * q:512 * q + 512], ps[:, 4 + q, :], bias, scale,
                                    ALU.add, ALU.mult).then_inc(proj_ev, 1)
                dve.wait_ge(proj_ev, n0 + 4)
                v.tensor_copy(parts[:, 0, :], qf).then_inc(split, 1)
                dve.wait_ge(split, s0 + 1)
                v.tensor_tensor(qf, qf, parts[:, 0, :], ALU.subtract).then_inc(split, 1)
                dve.wait_ge(split, s0 + 2)
                v.tensor_copy(parts[:, 1, :], qf).then_inc(split, 1)
                dve.wait_ge(split, s0 + 3)
                v.tensor_tensor(parts[:, 2, :], qf, parts[:, 1, :], ALU.subtract).then_inc(split, 1)

            normalise(0, xn0)
            project_and_split(0, 0, BQ, SCALE, qf0, qparts0)

            def k_rest(b, c):
                at, w = CUTS[c]
                dve.wait_ge(khi_done, count(lambda n: NCUT * n + c + 1, b))
                wait(dve, klo_done, count(lambda n: NCUT * n + c - 1, b))
                v.scalar_tensor_tensor(Krest[:, c % 2, 0:w], psM[:, 0:w], BK, Kpart[:, parity(b), 0, at:at + w],
                                       ALU.add, ALU.subtract).then_inc(krest_done, 1)
                dve.wait_ge(krest_done, count(lambda n: NCUT * n + c + 1, b))
                v.tensor_copy(Kpart[:, parity(b), 1, at:at + w], Krest[:, c % 2, 0:w]).then_inc(kmid_done, 1)

            def v_out(b, c):
                n = min(VT, MT - VT * c)
                w = 128 if c < NV - 1 else LAST_ROWS
                dve.wait_ge(bank_full, count(lambda k: USE["v", k, c] + 1, b))
                v.tensor_tensor(V[0:w, parity(b), VT * c:VT * c + n, :, 0:16],
                                psM[0:w, 0:128 * n].rearrange("p (m a k) -> p m a k", a=PAIRS, k=16),
                                bv4[0:w, 0:n, :].rearrange("p m (a k) -> p m a k", k=16),
                                ALU.add).then_inc(v_done, 1)

            def query_stack(b, g):
                u = units(b, g)
                wait(dve, s2_done, u(BLOCKS, -BLOCKS))
                for h in range(2):
                    last = v.tensor_scalar(Qst[0:ROWS, g, :, N * h:N * h + N],
                                           Qall[0:ROWS, GP * g:GP * g + GP, bass.ds(value(b) * N, N)],
                                           head_rows[0:ROWS, h:h + 1], None, ALU.mult)
                last.then_inc(qst_done, 1)

            def chunk_max(b, g, n):
                j, c = divmod(n, NCUT)
                dve.wait_ge(s1_done, units(b, g)(UC, n + 1))
                v.tensor_reduce(mxc[:, g, j, c:c + 1], psS1[:, n % 2, 0:CUTS[c][1]], AX.X, ALU.max)\
                 .then_inc(max_done, 1)

            def split_max(b, g):
                u = units(b, g)
                dve.wait_ge(max_done, u(UC, UC))
                v.tensor_reduce(nmf[:, g, :], mxc[:, g, :, :], AX.X, ALU.max, negate=True).then_inc(nm_chain, 1)
                dve.wait_ge(nm_chain, u(5, 1))
                v.tensor_copy(nmp[:, g, :, 0], nmf[:, g, :]).then_inc(nm_chain, 1)
                dve.wait_ge(nm_chain, u(5, 2))
                v.tensor_tensor(nmf[:, g, :], nmf[:, g, :], nmp[:, g, :, 0], ALU.subtract).then_inc(nm_chain, 1)
                dve.wait_ge(nm_chain, u(5, 3))
                v.tensor_copy(nmp[:, g, :, 1], nmf[:, g, :]).then_inc(nm_chain, 1)
                dve.wait_ge(nm_chain, u(5, 4))
                v.tensor_tensor(nmp[:, g, :, 2], nmf[:, g, :], nmp[:, g, :, 1], ALU.subtract).then_inc(nm_chain, 1)

            def read_out(b, g):
                dve.wait_ge(av_done, units(b, g)(BLOCKS, BLOCKS))
                v.tensor_copy(O[:, g, :], psO[:, 0:128]).then_inc(o_read, 1)

            def divide(b, g):
                u = units(b, g)
                wait_alone(dve, o_read, u(1, 1))
                v.stream_shuffle(den[:, g, :], O[:, g, :], SUM_ROWS).then_inc(norm_chain, 1)
                dve.wait_ge(norm_chain, u(2, 1))
                v.reciprocal(rden[:, g, :], den[:, g, :]).then_inc(norm_chain, 1)
                dve.wait_ge(norm_chain, u(2, 2))
                v.tensor_tensor(On[:, g, :], O[:, g, :], rden[:, g, :], ALU.mult).then_inc(norm_done, 1)

            def residual(b):
                dve.wait_ge(bank_full, count(lambda n: USE["y", n, 0] + 1, b))
                r = N * parity(b)
                m = bass.ds(value(b - parity(b)) // 2, 1) if isinstance(b, int) else bass.ds(b.i + b.off // 2, 1)
                x = x_all[r:r + N, m, :].rearrange("p o c -> p (o c)")
                v.tensor_tensor(x, psM[r:r + N, 0:C], x, ALU.add).then_inc(x1_done, 1)

            dve.wait_ge(w_in, 16 * N_W)
            for b in range(2):
                for c in range(NCUT):
                    k_rest(b, c)
            dve.wait_ge(pads, 6)
            for c in range(NV):
                v_out(0, c)
            dve.wait_ge(qst_in, 16 * SLOTS * PAIRS)
            query_stack(0, 0)
            for n in range(UC):
                chunk_max(0, 0, n)
            split_max(0, 0)

            def step(b, g):
                nxt, old = neighbour(b, g, 1), neighbour(b, g, -2)
                if there(old[0], 0, B):
                    read_out(*old)
                if there(nxt[0], 0, B):
                    query_stack(*nxt)
                if there(old[0], 0, B):
                    divide(*old)
                n = 0
                for s in range(BLOCKS):
                    if g == 1 and s == 1 and there(b, 1, B):
                        residual(b - 1)
                    for k in range(S1_AT[s]):
                        if there(nxt[0], 0, B):
                            chunk_max(*nxt, n)
                        n += 1
                        if g == 1 and 1 <= s <= NCUT:
                            if k == 0 and there(b, 0, B - 2):
                                k_rest(b + 2, s - 1)
                            if k == 1 and there(b, 0, B - 1):
                                v_out(b + 1, s - 1)
                if there(nxt[0], 0, B):
                    split_max(*nxt)

            def batch(b):
                for g in range(GROUPS):
                    step(b, g)

            over_batches(dve, batch)
            for g in range(GROUPS):
                read_out(B - 1, g)
                divide(B - 1, g)
            residual(B - 1)

            dve.wait_ge(x1_done, B)
            normalise(1, xn1)
            dve.wait_ge(sw_in, 16 * N_SW)
            dve.wait_ge(lora_pe, 1)
            for n in range(2):
                v.tensor_tensor(lw[:, 8 + n, :], ps[:, 4 + n, 0:128], lw[:, 7, :], ALU.mult).then_inc(lora_ev, 1)
            dve.wait_ge(lora_ev, 2)
            for n in range(2):
                v.scalar_tensor_tensor(lw[:, 5 + n, :], lw[:, 8 + n, :], LORA, ident[:],
                                       ALU.mult, ALU.add).then_inc(lora_ev, 1)
            dve.wait_ge(lora_pe, 2)
            v.tensor_copy(lw[:, 3, :], ps[:, 6, 0:128]).then_inc(lora_ev, 1)
            v.tensor_copy(lw[:, 4, :], ps[:, 6, 128:256]).then_inc(lora_ev, 1)
            v.tensor_copy(bv2[:], ps[:, 6, 256:384]).then_inc(lora_ev, 1)
            v.tensor_copy(SBQ2, ps[:, 6, 384:385]).then_inc(lora_ev, 1)
            dve.wait_ge(lora_ev, 8)
            project_and_split(4, 4, SBQ2, SCALE, qf1[:], qparts1)
            for q in range(4):
                dve.wait_ge(proj, 12 + q + 1)
                for j in range(4):
                    last = v.tensor_tensor(V2[:, 4 * q + j, :], ps[:, q, 128 * j:128 * j + 128], bv2[:], ALU.add)
                last.then_inc(vals, 1)
            dve.wait_ge(stack_in, 16 * SLOTS * PAIRS)
            dve.wait_ge(split, 8)
            project_and_split(8, 8, SBK, 1.0, qf1[:], qparts1)
            dve.wait_ge(stack_in, 16 * 2 * SLOTS * PAIRS)
            dve.wait_ge(pads, 9)

            def stacks(j, par):
                if isinstance(j, int):
                    if j >= 2:
                        dve.wait_ge(b_s2, j - 1)
                else:
                    dve.wait_ge(b_s2, j - 1)
                for e in range(2):
                    for h in range(2):
                        v.tensor_scalar(Q2st[0:ROWS, par, e, :, N * h:N * h + N],
                                        Qall[0:ROWS, :, bass.ds(j * 128 + N * e, N)],
                                        head_rows[0:ROWS, h:h + 1], None, ALU.mult)
                v.tensor_copy(K2st[0:ROWS, par, :, :], Kall[0:ROWS, :, bass.ds(j * 128, 128)]).then_inc(b_st, 1)

            def maxima(j, par):
                dve.wait_ge(b_s1, j + 1)
                v.tensor_reduce(nmf2[:, par, :], ps[:, 0:2, :].rearrange("p e (a m) -> p (e a) m", m=N), AX.X,
                                ALU.max, negate=True).then_inc(b_chain, 1)
                dve.wait_ge(b_chain, j * 5 + 1)
                v.tensor_copy(nmp2[:, par, :, 0], nmf2[:, par, :]).then_inc(b_chain, 1)
                dve.wait_ge(b_chain, j * 5 + 2)
                v.tensor_tensor(nmf2[:, par, :], nmf2[:, par, :], nmp2[:, par, :, 0], ALU.subtract).then_inc(b_chain, 1)
                dve.wait_ge(b_chain, j * 5 + 3)
                v.tensor_copy(nmp2[:, par, :, 1], nmf2[:, par, :]).then_inc(b_chain, 1)
                dve.wait_ge(b_chain, j * 5 + 4)
                v.tensor_tensor(nmp2[:, par, :, 2], nmf2[:, par, :], nmp2[:, par, :, 1], ALU.subtract)\
                 .then_inc(b_chain, 1)

            def pair(j, par, more=True):
                if more:
                    stacks(j + 1, 1 - par)
                    maxima(j + 1, 1 - par)
                wait_alone(dve, b_av, j + 1)
                o = ps[:, 6:8, 0:2 * 128]
                v.stream_shuffle(den2[:].rearrange("p (e g) b -> p e (g b)", e=2), o, SUM_ROWS).then_inc(b_norm, 1)
                dve.wait_ge(b_norm, j * 3 + 1)
                v.reciprocal(rden2[:].rearrange("p a b -> p (a b)"), den2[:].rearrange("p a b -> p (a b)"))\
                 .then_inc(b_norm, 1)
                dve.wait_ge(b_norm, j * 3 + 2)
                v.tensor_tensor(On2[:].rearrange("p (e g) b -> p e (g b)", e=2), o,
                                rden2[:].rearrange("p (e g) b -> p e (g b)", e=2), ALU.mult).then_inc(b_norm, 1)
                dve.wait_ge(b_y, j + 1)
                v.tensor_tensor(ytmp[:], ps[:, 2, 0:C], bp[:], ALU.add).then_inc(b_xa, 1)
                dve.wait_ge(b_xa, j + 1)
                x = x_all[:, bass.ds(j, 1), :].rearrange("p o c -> p (o c)")
                v.tensor_tensor(x, x, ytmp[:], ALU.add).then_inc(b_x, 1)

            stacks(0, 0)
            maxima(0, 0)
            pair(0, 0)
            with dve.Fori(0, (TILES - 2) // 2) as i:
                pair(i * 2 + 1, 1)
                pair(i * 2 + 2, 0)
            pair(TILES - 1, 1, more=False)

            dve.wait_ge(b_x, TILES)
            normalise(2, xn1)
            dve.wait_ge(fw_in, 16 * 5)
            dve.wait_ge(g_pe, 1)
            v.tensor_copy(gs[:].rearrange("p a b -> p (a b)"), ps[:, 4, 0:8 * TILES]).then_inc(g_chain, 1)
            dve.wait_ge(g_chain, 1)
            for m in range(TILES):
                last = v.max(top[:, m, :], gs[:, m, :])
            last.then_inc(g_chain, 1)
            dve.wait_ge(g_chain, 2)
            for m in range(TILES):
                last = v.max_index(topi[:, m, :], top[:, m, :], gs[:, m, :])
            last.then_inc(g_chain, 1)
            dve.wait_ge(g_chain, 3)
            v.tensor_copy(topf[:], topi[:])
            v.tensor_tensor(tw[:, 0, :], top[:, :, 1], top[:, :, 0], ALU.subtract).then_inc(g_chain, 1)
            dve.wait_ge(g_exp, 1)
            v.tensor_scalar(tw[:, 2, :], tw[:, 1, :], 1.0, None, ALU.add).then_inc(g_chain, 1)
            dve.wait_ge(g_chain, 5)
            v.reciprocal(tw[:, 2, :], tw[:, 2, :]).then_inc(g_chain, 1)
            dve.wait_ge(g_chain, 6)
            v.tensor_tensor(tw[:, 3, :], tw[:, 1, :], tw[:, 2, :], ALU.mult).then_inc(g_chain, 1)
            dve.wait_ge(g_chain, 7)
            for m in range(TILES):
                v.tensor_scalar(comb[:, m, :], iota[:], topf[:, m, 0:1], tw[:, 2, m:m + 1], ALU.is_equal, ALU.mult)
                last = v.tensor_scalar(comb2[:, m, :], iota[:], topf[:, m, 1:2], tw[:, 3, m:m + 1],
                                       ALU.is_equal, ALU.mult)
            last.then_inc(g_chain, 1)
            dve.wait_ge(g_chain, 8)
            v.tensor_tensor(comb[:], comb[:], comb2[:], ALU.add).then_inc(g_chain, 1)
            dve.wait_ge(g_chain, 9)

            def hidden(q, e, m):
                n = q * (EXPERTS * HT) + (HT * e + m)
                dve.wait_ge(h_sil, n + 1)
                if not isinstance(n, int) or n >= 2 * HT:
                    dve.wait_ge(y_pe, q * EXPERTS + e - 1)
                v.tensor_tensor(hT[:, e % 2, m, :], ps[:, 2 + m % 2, :], sil[:, m % 2, :], ALU.mult).then_inc(h_done, 1)

            def add_expert(q, e):
                n = q * EXPERTS + e
                dve.wait_ge(y_pe, n + 1)
                if isinstance(n, int):
                    wait(dve, y_done, n)
                else:
                    dve.wait_ge(y_done, n)
                for k in range(CT):
                    w = comb[:, bass.ds(q * CT + k, 1), e:e + 1].rearrange("p o e -> p (o e)")
                    before = x_all[:, bass.ds(q * CT + k, 1), :].rearrange("p o c -> p (o c)") if e == 0 else \
                        acc[:, (e + 1) % 2, k, :]
                    last = v.scalar_tensor_tensor(acc[:, e % 2, k, :], ps[:, 5 + e % 2, 128 * k:128 * k + 128], w,
                                                  before, ALU.mult, ALU.add)
                last.then_inc(y_done, 1)

            def finish(q, par):
                add_expert(q, EXPERTS - 1)
                dve.wait_ge(y_done, q * EXPERTS + EXPERTS)
                wait(dve, o_out[par], 16 * (q // 2))
                v.tensor_copy(out_t[:, par], acc[:, (EXPERTS - 1) % 2]).then_inc(o_done, 1)

            def chunk_with(q, before, par):
                for e in range(EXPERTS):
                    for m in range(HT):
                        hidden(q, e, m)
                        if m == 1:
                            if e:
                                add_expert(q, e - 1)
                            elif before is not None:
                                finish(before, par)

            for q in range(CHUNKS):
                chunk_with(q, q - 1 if q else None, (q - 1) % 2)
            finish(CHUNKS - 1, (CHUNKS - 1) % 2)


def kernel(**inputs):
    import concourse.bacc as bacc
    from concourse.bass_utils import run_bass_kernel_spmd as run

    g = {k: np.asarray(v) for k, v in inputs.items()}
    xa, at, ff = "L0_xattn_", "L0_attn_", "L0_ffn_"

    def by_pair(w):
        o = np.zeros((GP, 32, GROUPS, 2, C), w.dtype)
        w = w.reshape(GROUPS, GP, 2, D, C)
        for h in range(2):
            o[:, D * h:D * h + D, :, h, :] = w[:, :, h].transpose(1, 2, 0, 3)
        return o.reshape(128, GROUPS, 2, C)

    wqkv, bqkv = g[at + "w_qkv"], g[at + "b_qkv"].reshape(3, C, 1)
    rows = np.arange(128)
    f = np.float32
    arrays = {
        "x": g["x"].reshape(T, C), "ctxT": g["ctx_1024"].transpose(0, 2, 1),
        "WqT": g[xa + "Wq"].T, "WkT": g[xa + "Wk"].T, "WvT": g[xa + "Wv"].T, "WoP": by_pair(g[xa + "Wo"].T),
        "bq": g[xa + "bq"].reshape(C, 1), "bk": g[xa + "bk"].reshape(C, 1), "bv": g[xa + "bv"].reshape(1, C),
        "wqT": wqkv[:, 0:C].T, "wk": wqkv[:, C:2 * C], "wvT": wqkv[:, 2 * C:].T,
        "sbq": bqkv[0], "sbk": bqkv[1], "sbv": np.tile(bqkv[2], (1, 128)),
        "aqT": np.tile(g[at + "a_q"].T, (1, H)), "bbq": np.tile(g[at + "b_q"], (1, H)),
        "avT": np.tile(g[at + "a_v"].T, (1, H)), "bbv": np.tile(g[at + "b_v"], (1, H)),
        "WpP": by_pair(g[at + "w_proj"]), "bp": g[at + "b_proj"].reshape(1, C),
        "gateT": g[ff + "gate_w"].T, "W1T": g[ff + "w1"].transpose(2, 0, 1), "W3T": g[ff + "w3"].transpose(2, 0, 1),
        "W2T": g[ff + "w2"].transpose(2, 0, 1).reshape(HT, 128, EXPERTS, C).transpose(1, 2, 0, 3),
        "ident": np.eye(128, dtype=f), "head_rows": (rows[:, None] // D % 2 == np.arange(2)).astype(f),
        "head_block": (rows[:, None] // D == rows // D).astype(f),
        "iota": np.tile(np.arange(EXPERTS, dtype=f), (128, 1)),
    }
    nc = bacc.Bacc("TRN2", target_bir_lowering=False, num_devices=1)
    t = {}
    for name, shape in INS.items():
        arrays[name] = np.ascontiguousarray(arrays[name])
        assert arrays[name].shape == shape, name
        t[name] = nc.dram_tensor("in_" + name, shape, F32, kind="ExternalInput").ap()
    out = nc.dram_tensor("out", (T, C), F32, kind="ExternalOutput").ap()
    perceiver(nc, t, out)
    r = run(nc, [{"in_" + n: a for n, a in arrays.items()}], core_ids=[0])
    return r.results[0]["out"].reshape(B, N, C)
```

```python
from contextlib import ExitStack

import concourse.bass as bass
from concourse import mybir
import numpy as np

F32 = mybir.dt.float32
BF16 = mybir.dt.bfloat16
U32 = mybir.dt.uint32
ALU = mybir.AluOpType
ACT = mybir.ActivationFunctionType
AX = mybir.AxisListType

B, N, C = 32, 64, 128
M = 1601
H, D = 16, 8
T = B * N
TILES = T // 128
PAIRS = H // 2
GROUPS = 2
GP = PAIRS // GROUPS
MT = -(-M // 128)
MPAD = MT * 128
LAST_ROWS = M - 128 * (MT - 1)
K_PART = [0, 0, 0, 1, 1, 2]
Q_PART = [0, 1, 2, 0, 1, 0]
SLOTS = len(K_PART)
ROWS = SLOTS * 2 * D
CUTS = [(0, 402), (402, 400), (802, 400), (1202, 399)]
NCUT = len(CUTS)
UC = GP * NCUT
S1_AT = [1, 1, 1, 2, 1, 1, 1, 2, 1, 1, 1, 2, 1]
S1_AHEAD = UC // 2
M_AT = 8
K_AT = {2: 0, 4: 1, 7: 2, 9: 3}
KMID_AT = {5: 0, 7: 1, 10: 2, 12: 3}
V_AT = {0: 0, 2: 1, 4: 2, 6: 3}
QST_AT = 3
Y_AT = 10
S2_BACK = [[2, 2, 5] + [3] * (MT - 3), [3] * MT]
VT = 4
NV = -(-MT // VT)
EXPERTS, HID, TOPK = 8, 512, 2
HT = HID // 128
CHUNK = 512
CHUNKS = T // CHUNK
CT = CHUNK // 128
EPS = 1e-5
SCALE = float(D) ** -0.5
LORA = 2.0
R = 16
LN_STEPS = 4
SUM_ROWS = [16 + n % 16 for n in range(32)]
N_SW = 13
FIRST, LAST = 1, B // 2 - 3

INS = {
    "x": (T, C), "ctxT": (B, C, M), "WqT": (C, C), "WkT": (C, C), "WvT": (C, C), "WoP": (128, GROUPS, 2, C), "WoT": (C, C),
    "bq": (C, 1), "bk": (C, 1), "bv": (C, 128), "wqT": (C, C), "wk": (C, C), "wvT": (C, C),
    "sbq": (C, 1), "sbk": (C, 1), "sbv": (C, 128), "aqT": (R, C), "bbq": (R, C), "avT": (R, C), "bbv": (R, C),
    "WpP": (128, GROUPS, 2, C), "bp": (1, C), "gateT": (C, EXPERTS), "W1T": (C, EXPERTS, HID),
    "W3T": (C, EXPERTS, HID), "W2T": (128, EXPERTS, HT, C),
    "ident": (128, 128), "head_rows": (128, 2), "head_block": (128, 128), "iota": (128, EXPERTS),
}


class Batch:

    def __init__(self, i, off):
        self.i, self.off = i, off

    def __add__(self, k):
        return Batch(self.i, self.off + k)

    def __sub__(self, k):
        return Batch(self.i, self.off - k)


def parity(b):
    return (b if isinstance(b, int) else b.off) % 2


def value(b):
    return b if isinstance(b, int) else b.i * 2 + b.off


def count(f, b):
    if isinstance(b, int):
        return f(b)
    slope = f(b.off + 2 * FIRST + 2) - f(b.off + 2 * FIRST)
    return b.i * slope + (f(b.off + 2 * FIRST) - slope * FIRST)


def uses():
    out = [("v", 0, c) for c in range(NV)] + [("m", 0, 0)]
    for b in range(B):
        for g in range(GROUPS):
            for s in range(MT):
                if s == M_AT and (g == 0 or b + 1 < B):
                    out.append(("m", b + g, 1 - g))
                if g == 1 and s == Y_AT and b:
                    out.append(("y", b - 1, 0))
                if g == 1 and s in V_AT and b + 1 < B:
                    out.append(("v", b + 1, V_AT[s]))
    out.append(("y", B - 1, 0))
    return out


ORDER = uses()
USE = {u: n for n, u in enumerate(ORDER)}


def perceiver(nc, t, out):
    ctx = ExitStack()
    scope = ExitStack()

    def sb(name, shape, dt=F32, where=ctx):
        return where.enter_context(nc.sbuf_tensor(name, shape, dt))

    def sem(name):
        return ctx.enter_context(nc.semaphore(name))

    def wait(eng, s, v):
        if not isinstance(v, int) or v > 0:
            eng.wait_ge(s, v)

    with ctx:
        x_all = sb("x_all", [128, TILES, C])
        ident = sb("ident_sb", [128, 128])
        identb = sb("identb", [128, 128], BF16)
        head_rows = sb("head_rows_sb", [128, 2])
        eps = sb("eps", [128, 1])
        stats = sb("stats", [128, TILES, 6])
        mv = sb("mv", [128, TILES, 2])
        std = sb("std", [128, TILES])
        rstd = sb("rstd", [128, TILES])
        biases = sb("biases", [128, 8])
        BQ, BK, SBQ, SBK, SBV, SBQ2 = (biases[:, n:n + 1] for n in range(6))
        WqT, WkT, WvT = (sb(n, [128, 128]) for n in ("WqT_sb", "WkT_sb", "WvT_sb"))
        WoP = sb("WoP_sb", [128, GROUPS, 2, C])
        bo = sb("bo", [128, C])
        Qall = sb("Qall", [128, PAIRS, T], BF16)

        Kst = sb("Kst", [128, 2, PAIRS, MPAD], BF16, scope)
        Kpart = sb("Kpart", [128, 2, 3, M], BF16, scope)
        Krest = sb("Krest", [128, 2, CUTS[0][1]], F32, scope)
        V = sb("V", [128, 2, MT, PAIRS, 32], F32, scope)
        P = sb("P", [128, MT + 1, 512], F32, scope)
        ctxT = sb("ctxT_sb", [128, 2, M], F32, scope)
        Qst = sb("Qst", [128, 2, GROUPS, GP, 128], BF16, scope)
        mxc = sb("mxc", [128, 2, GP, NCUT], F32, scope)
        nmf = sb("nmf", [128, 2, GP], F32, scope)
        nmp = sb("nmp", [128, 2, GP, 3], BF16, scope)
        den = sb("den", [128, 2, 128], F32, scope)
        O = sb("O", [128, 2, 128], F32, scope)
        WoT = sb("WoT_sb", [128, 128], F32, scope)
        bvc = sb("bvc", [128, 128], F32, scope)
        On = sb("On", [128, 2, 128], F32, scope)
        xnT0 = P[:, 0:4, :].rearrange("p a b -> p (a b)")
        qf0 = P[:, 4:8, :].rearrange("p a b -> p (a b)")
        qparts0 = P[:, 8:14, :].rearrange("p a b -> p (a b)").bitcast(BF16).rearrange("p (k t) -> p k t", k=3)
        xn0 = V[:, 0, 0:8, :, :].rearrange("p a b c -> p (a b c)").rearrange("p (t c) -> p t c", c=C)
        scope.close()

        W1T = sb("W1T_sb", [128, EXPERTS, HID])
        W3T = sb("W3T_sb", [128, EXPERTS, HID])
        W2T = sb("W2T_sb", [128, EXPERTS, HT, C])
        gateT = sb("gateT_sb", [128, EXPERTS])
        iota = sb("iota_sb", [128, EXPERTS])
        xn1 = sb("xn1", [128, TILES, C])
        xnT1 = sb("xnT1", [128, T])
        scope2 = ExitStack()
        Kall = sb("Kall", [128, PAIRS, T], BF16, scope2)
        qf1 = sb("qf1", [128, T], F32, scope2)
        qparts1 = sb("qparts1", [128, 3, T], BF16, scope2)
        V2 = sb("V2", [128, TILES, C], F32, scope2)
        V2st = sb("V2st", [128, 2, PAIRS, 32], F32, scope2)
        P2 = sb("P2", [128, PAIRS, 128], F32, scope2)
        K2st = sb("K2st", [128, 2, PAIRS, 128], BF16, scope2)
        Q2st = sb("Q2st", [128, 2, 2, PAIRS, 128], BF16, scope2)
        lw = sb("lw", [128, 10, 128], F32, scope2)
        lora = sb("lora", [R, 4, C], F32, scope2)
        sbvc = sb("sbvc", [128, 128], F32, scope2)
        bv2 = sb("bv2", [128, C], F32, scope2)
        bp = sb("bp_sb", [128, C], F32, scope2)
        WpP = sb("WpP_sb", [128, GROUPS, 2, C], F32, scope2)
        nmf2 = sb("nmf2", [128, 2, 16], F32, scope2)
        nmp2 = sb("nmp2", [128, 2, 16, 3], BF16, scope2)
        den2 = sb("den2", [128, 4, 128], F32, scope2)
        rden2 = sb("rden2", [128, 4, 128], F32, scope2)
        On2 = sb("On2", [128, 4, 128], F32, scope2)
        ytmp = sb("ytmp", [128, C], F32, scope2)
        scope2.close()
        gs = sb("gs", [128, TILES, 8])
        top = sb("top", [128, TILES, 8])
        topi = sb("topi", [128, TILES, 8], U32)
        topf = sb("topf", [128, TILES, 8])
        tw = sb("tw", [128, 4, TILES])
        comb = sb("comb", [128, TILES, EXPERTS])
        comb2 = sb("comb2", [128, TILES, EXPERTS])
        sil = sb("sil", [128, 2, CHUNK])
        hT = sb("hT", [128, 2, HT, CHUNK])
        acc = sb("acc", [128, 2, CT, C])
        out_t = sb("out_t", [128, 2, CT, C])

        ps = ctx.enter_context(nc.psum_tensor("ps", [128, 8, 512], F32))
        psS1 = ps[:, 0:2, :]
        psS2 = ps[:, 2:5, :]
        psK = ps[:, 5, :]
        psO = ps[:, 6, :]
        psM = ps[:, 7, :]

        load = sem("load")
        w_in = sem("w_in")
        sw_in = sem("sw_in")
        fw_in = sem("fw_in")
        made = sem("made")
        pads = sem("pads")
        ctx_in = [sem(f"ctx_in{n}") for n in range(2)]
        kst_in = [[sem(f"kst_in{n}{g}") for g in range(GROUPS)] for n in range(2)]
        qst_in = sem("qst_in")
        s1_done = sem("s1_done")
        s2_done = sem("s2_done")
        av_done = sem("av_done")
        k_full = sem("k_full")
        bank_full = sem("bank_full")
        exp_done = sem("exp_done")
        kf_done = sem("kf_done")
        khi_done = sem("khi_done")
        max_rows = sem("max_rows")
        max_done = sem("max_done")
        nm_chain = sem("nm_chain")
        o_read = sem("o_read")
        den_done = sem("den_done")
        norm_done = sem("norm_done")
        qst_done = sem("qst_done")
        krest_done = sem("krest_done")
        kmid_done = sem("kmid_done")
        klo_done = sem("klo_done")
        kd_in = [sem(f"kd_in{n}") for n in range(2)]
        qd_in = sem("qd_in")
        bo_pe = sem("bo_pe")
        bo_done = sem("bo_done")
        v_done = sem("v_done")
        x1_done = sem("x1_done")
        ln_stat = sem("ln_stat")
        ln_std = sem("ln_std")
        ln_tr = sem("ln_tr")
        ln_ev = sem("ln_ev")
        proj = sem("proj")
        proj_ev = sem("proj_ev")
        split = sem("split")
        stack_in = sem("stack_in")
        lora_pe = sem("lora_pe")
        lora_ev = sem("lora_ev")
        b_st = sem("b_st")
        b_s1 = sem("b_s1")
        b_chain = sem("b_chain")
        b_nm = sem("b_nm")
        b_rows = sem("b_rows")
        b_s2 = sem("b_s2")
        b_exp = sem("b_exp")
        b_v = sem("b_v")
        b_av = sem("b_av")
        b_norm = sem("b_norm")
        b_y = sem("b_y")
        vals = sem("vals")
        b_xa = sem("b_xa")
        b_x = sem("b_x")
        g_pe = sem("g_pe")
        g_chain = sem("g_chain")
        g_exp = sem("g_exp")
        h_pe = sem("h_pe")
        h_sil = sem("h_sil")
        h_done = sem("h_done")
        y_pe = sem("y_pe")
        y_done = sem("y_done")
        o_done = sem("o_done")
        o_out = [sem(f"o_out{n}") for n in range(2)]

        def wait_alone(eng, s, v):
            v = v if isinstance(v, int) else eng.snap(eng.to_reg(v))
            eng.wait_ge(load, 16)
            wait(eng, s, v)

        N_LOAD, N_W = 4, 7
        kd = nc.dram_tensor("k_parts", (2, 3, 128, M), BF16, kind="Internal").ap()
        qd = nc.dram_tensor("q_parts", (3, 128, T), BF16, kind="Internal").ap()
        block = ctx.enter_context(nc.Block())

        def over_batches(eng, body):
            for b in range(2 * FIRST):
                body(b)
            with eng.Fori(FIRST, LAST + 1) as i:
                for off in range(2):
                    body(Batch(i, off))
            for b in range(2 * LAST + 2, B):
                body(b)

        def there(b, lo, hi):
            return lo <= b < hi if isinstance(b, int) else True

        def units(b, g):
            return lambda k, add: count(lambda n: k * (2 * n + g) + add, b)

        def neighbour(b, g, k):
            n = g + k
            return b + n // 2, n % 2

        def s1_chunks(b, g):
            return [(*neighbour(b, g, 1), n) for n in range(S1_AHEAD, UC)] + \
                   [(*neighbour(b, g, 2), n) for n in range(S1_AHEAD)]

        @block.sync
        def _(sp):
            sp.dma_start(x_all[:], t["x"].rearrange("(n p) c -> p n c", p=128)).then_inc(load, 16)
            sp.dma_start(ident[:], t["ident"]).then_inc(load, 16)
            sp.dma_start(head_rows[:], t["head_rows"]).then_inc(load, 16)
            sp.dma_start(BQ, t["bq"]).then_inc(load, 16)
            sp.dma_start(WqT[:], t["WqT"]).then_inc(w_in, 16)
            sp.dma_start(WkT[:], t["WkT"]).then_inc(w_in, 16)
            sp.dma_start(BK, t["bk"]).then_inc(w_in, 16)
            sp.dma_start(ctxT[:, 0, :], t["ctxT"][0]).then_inc(ctx_in[0], 16)
            sp.dma_start(ctxT[:, 1, :], t["ctxT"][1]).then_inc(ctx_in[1], 16)
            sp.dma_start(WvT[:], t["WvT"]).then_inc(w_in, 16)
            sp.dma_start(WoP[:], t["WoP"]).then_inc(w_in, 16)
            sp.dma_start(bvc[:], t["bv"]).then_inc(w_in, 16)
            sp.dma_start(WoT[:], t["WoT"]).then_inc(w_in, 16)

            def stack_all(s0, d0, parts, part_of, dst, done):
                for part in range(3):
                    sp.wait_ge(split, s0 + [1, 3, 4][part])
                    sp.dma_start(qd[part], parts[:, part, :]).then_inc(qd_in, 16)
                    sp.wait_ge(qd_in, 16 * (d0 + part + 1))
                    for s in range(SLOTS):
                        if part_of[s] == part:
                            sp.dma_start(dst[16 * s:16 * s + 16, :, :],
                                         qd[part].rearrange("(p r) t -> r p t", r=16)).then_inc(done, 16)

            stack_all(0, 0, qparts0, Q_PART, Qall, qst_in)

            def parts_out(b):
                for c, (at, w) in enumerate(CUTS):
                    wait_alone(sp, klo_done, count(lambda n: NCUT * n + c + 1, b))
                    sp.dma_start(kd[parity(b)].rearrange("k r m -> r k m")[:, :, at:at + w],
                                 Kpart[:, parity(b), :, at:at + w]).then_inc(kd_in[parity(b)], 16)
                wait_alone(sp, kd_in[parity(b)], count(lambda n: 16 * NCUT * (n // 2 + 1), b))

            def k_stack(b, g):
                if there(b, 2, B):
                    wait_alone(sp, s2_done, count(lambda n: MT * (2 * (n - 2) + g + 1), b))
                for s in range(SLOTS):
                    sp.dma_start(Kst[16 * s:16 * s + 16, parity(b), GP * g:GP * g + GP, 0:M],
                                 kd[parity(b), K_PART[s], 64 * g:64 * g + 64].rearrange("(p r) m -> r p m", r=16))\
                      .then_inc(kst_in[parity(b)][g], 16)

            def context(b):
                wait_alone(sp, bank_full, count(lambda n: 1 + USE["v", n, NV - 1], b - 2))
                sp.dma_start(ctxT[:, parity(b), :],
                             t["ctxT"][bass.ds(value(b), 1)].rearrange("o c m -> (o c) m"))\
                  .then_inc(ctx_in[parity(b)], 16)

            parts_out(0)
            for g in range(GROUPS):
                k_stack(0, g)
            context(2)
            parts_out(1)
            for g in range(GROUPS):
                k_stack(1, g)

            def batch(b):
                if there(b, 0, B - 2):
                    parts_out(b + 2)
                    k_stack(b + 2, 0)
                if there(b, 0, B - 3):
                    context(b + 3)
                if there(b, 0, B - 2):
                    k_stack(b + 2, 1)

            over_batches(sp, batch)

            sp.wait_ge(x1_done, B)
            for n, name in enumerate(("wqT", "wk", "wvT")):
                sp.dma_start(lw[:, n, :], t[name]).then_inc(sw_in, 16)
            sp.dma_start(lw[:, 7, :], t["head_block"]).then_inc(sw_in, 16)
            for n, name in enumerate(("aqT", "bbq", "avT", "bbv")):
                sp.dma_start(lora[:, n, :], t[name]).then_inc(sw_in, 16)
            sp.dma_start(SBQ, t["sbq"]).then_inc(sw_in, 16)
            sp.dma_start(SBK, t["sbk"]).then_inc(sw_in, 16)
            sp.dma_start(sbvc[:], t["sbv"]).then_inc(sw_in, 16)
            sp.dma_start(WpP[:], t["WpP"]).then_inc(sw_in, 16)
            sp.dma_start(bp[:], t["bp"].to_broadcast((128, C))).then_inc(sw_in, 16)
            for name, dst in (("gateT", gateT), ("iota", iota), ("W1T", W1T), ("W3T", W3T), ("W2T", W2T)):
                sp.dma_start(dst[:], t[name]).then_inc(fw_in, 16)
            stack_all(4, 3, qparts1, Q_PART, Qall, stack_in)
            stack_all(8, 6, qparts1, K_PART, Kall, stack_in)
            with sp.Fori(0, CHUNKS // 2) as i:
                for k in range(2):
                    wait_alone(sp, o_done, i * 2 + k + 1)
                    sp.dma_start(out[bass.ds(i * (2 * CHUNK) + k * CHUNK, CHUNK), :].rearrange("(n p) c -> p n c", p=128),
                                 out_t[:, k]).then_inc(o_out[k], 16)
            for k in range(2):
                sp.wait_ge(o_out[k], 16 * (CHUNKS // 2))

        @block.gpsimd
        def _(pool):
            for n in range(2):
                nc.gpsimd.memset(Kst[96:99, n, :, :], 1.0).then_inc(pads, 1)
                pool.wait_ge(pads, 2 * n + 1)
                nc.gpsimd.memset(Kst[0:96, n, :, M:MPAD], 0.0).then_inc(pads, 1)
                pool.wait_ge(pads, 2 * n + 2)
            pool.wait_ge(ln_tr, TILES // 4)
            for n in range(2):
                nc.gpsimd.memset(V[:, n, :, :, 16:32], 1.0).then_inc(pads, 1)
                pool.wait_ge(pads, n + 5)

            def k_parts(b, c):
                at, w = CUTS[c]
                done = count(lambda n: NCUT * n + c + 1, b)
                pool.wait_ge(kf_done, done)
                nc.gpsimd.tensor_tensor(Krest[:, c % 2, 0:w], Krest[:, c % 2, 0:w], Kpart[:, parity(b), 0, at:at + w],
                                        ALU.subtract).then_inc(krest_done, 1)
                pool.wait_ge(kmid_done, done)
                nc.gpsimd.tensor_tensor(Kpart[:, parity(b), 2, at:at + w], Krest[:, c % 2, 0:w],
                                        Kpart[:, parity(b), 1, at:at + w], ALU.subtract).then_inc(klo_done, 1)
                pool.wait_ge(klo_done, done)

            def divide(b, g):
                pool.wait_ge(den_done, units(b, g)(2, 2))
                nc.gpsimd.tensor_tensor(On[:, g, :], O[:, g, :], den[:, g, :], ALU.mult).then_inc(norm_done, 1)
                pool.wait_ge(norm_done, units(b, g)(1, 1))

            for b in range(2):
                for c in range(NCUT):
                    k_parts(b, c)

            def batch(b):
                if there(b, 1, B):
                    divide(b - 1, 0)
                if there(b, 0, B - 2):
                    for c in range(NCUT):
                        k_parts(b + 2, c)
                if there(b, 1, B):
                    divide(b - 1, 1)

            over_batches(pool, batch)
            for g in range(GROUPS):
                divide(B - 1, g)
            pool.wait_ge(x1_done, B)
            nc.gpsimd.memset(V2st[:, :, :, 16:32], 1.0).then_inc(pads, 1)
            for n in range(2):
                pool.wait_ge(pads, n + 7)
                nc.gpsimd.memset(K2st[96:99, n, :, :], 1.0).then_inc(pads, 1)

        @block.tensor
        def _(pe):
            mm = nc.tensor.matmul

            def turn_tiles(k, xn):
                pe.wait_ge(ln_stat, LN_STEPS * (k + 1))
                for q in range(TILES // 4):
                    n = k * (TILES // 4) + q
                    for j in range(4):
                        last = nc.tensor.transpose(ps[:, q % 4, 128 * j:128 * j + 128], xn[:, 4 * q + j, :], ident[:])
                    last.then_inc(ln_tr, 1)

            turn_tiles(0, xn0)
            pe.wait_ge(w_in, 16 * N_W)
            for q in range(4):
                pe.wait_ge(ln_ev, q + 1)
                mm(ps[:, 4 + q, :], WqT[:], xnT0[:, 512 * q:512 * q + 512], start=True, stop=True).then_inc(proj, 1)

            def bank(kind, b, c):
                some = b if isinstance(b, int) else b.off + 2 * FIRST
                if USE[kind, some, c] == 0:
                    return
                last, bb, cc = ORDER[USE[kind, some, c] - 1]
                read, of_batch = {"v": (v_done, NV), "m": (max_rows, GROUPS), "y": (x1_done, 1)}[last]
                pe.wait_ge(read, count(lambda n: of_batch * (n + bb - some) + cc + 1, b))

            def k_chunk(b, c):
                at, w = CUTS[c]
                wait(pe, kf_done, count(lambda n: NCUT * n + c, b))
                if c == 0:
                    pe.wait_ge(ctx_in[parity(b)], count(lambda n: 16 * (n // 2 + 1), b))
                mm(psK[:, 0:w], WkT[:], ctxT[:, parity(b), at:at + w], start=True, stop=True).then_inc(k_full, 1)

            def v_chunk(b, c):
                bank("v", b, c)
                if c == 0:
                    pe.wait_ge(ctx_in[parity(b)], count(lambda n: 16 * (n // 2 + 1), b))
                for m in range(VT * c, min(VT * c + VT, MT)):
                    w = 128 if m < MT - 1 else LAST_ROWS
                    last = mm(psM[0:w, 128 * (m - VT * c):128 * (m - VT * c) + 128],
                              ctxT[:, parity(b), 128 * m:128 * m + w], WvT[:], start=True, stop=True)
                last.then_inc(bank_full, 1)

            def s1(b, g, n):
                u = units(b, g)
                j, c = divmod(n, NCUT)
                at, w = CUTS[c]
                if n == 0:
                    pe.wait_ge(qst_done, u(1, 1))
                    pe.wait_ge(kst_in[parity(b)][g], count(lambda k: 16 * SLOTS * (k // 2 + 1), b))
                wait(pe, max_done, u(UC, n - 1))
                mm(psS1[:, n % 2, 0:w], Qst[0:ROWS, parity(b), g, j, :], Kst[0:ROWS, parity(b), GP * g + j, at:at + w],
                   start=True, stop=True).then_inc(s1_done, 1)

            def max_to_rows(b, g):
                bank("m", b, g)
                pe.wait_ge(nm_chain, units(b, g)(5, 5))
                for j in range(GP):
                    last = mm(psM[96:99, 128 * j:128 * j + 128], nmp[:, g, j, :], identb[:], start=True, stop=True)
                last.then_inc(bank_full, 1)

            def s2(b, g, m):
                u = units(b, g)
                if m == 0:
                    pe.wait_ge(max_rows, u(1, 1))
                wait(pe, exp_done, u(MT, m + 1 - S2_BACK[g][m]))
                for j in range(GP):
                    last = mm(psS2[:, (m + g) % 3, 128 * j:128 * j + 128],
                              Kst[0:ROWS + 3, parity(b), GP * g + j, 128 * m:128 * m + 128],
                              Qst[0:ROWS + 3, parity(b), g, j, :], start=True, stop=True)
                last.then_inc(s2_done, 1)

            def av(b, g, m):
                u = units(b, g)
                if m == 0:
                    pe.wait_ge(v_done, count(lambda n: NV * (n + 1), b))
                    wait(pe, o_read, u(1, 0))
                pe.wait_ge(exp_done, u(MT, m + 1))
                w = 128 if m < MT - 1 else LAST_ROWS
                for j in range(GP):
                    last = mm(psO[32 * j:32 * j + 32, 0:128], V[0:w, parity(b), m, GP * g + j, :],
                              P[0:w, m, 128 * j:128 * j + 128], start=(m == 0), stop=(m == MT - 1))
                last.then_inc(av_done, 1)

            def project_out(b):
                bank("y", b, 0)
                pe.wait_ge(norm_done, units(b, 1)(1, 1))
                r = N * parity(b)
                for g in range(GROUPS):
                    for h in range(2):
                        last = mm(psM[r:r + N, 0:C], On[:, g, N * h:N * h + N], WoP[:, g, h, :],
                                  start=(g == 0 and h == 0), stop=(g == 1 and h == 1))
                last.then_inc(bank_full, 1)

            pe.wait_ge(proj_ev, 4)
            mm(ps[:, 4, 0:128], bvc[:], WoT[:], start=True, stop=True).then_inc(bo_pe, 1)
            for b in range(2):
                for c in range(NCUT):
                    k_chunk(b, c)
            for c in range(NV):
                v_chunk(0, c)
            pe.wait_ge(pads, 6)
            pe.wait_ge(made, 1)
            for n in range(UC):
                s1(0, 0, n)
            max_to_rows(0, 0)
            for n in range(S1_AHEAD):
                s1(0, 1, n)

            def step(b, g):
                prev, nxt = neighbour(b, g, -1), neighbour(b, g, 1)
                todo = s1_chunks(b, g)
                for m in range(MT):
                    s2(b, g, m)
                    if m and there(prev[0], 0, B):
                        for k in ([0, 1] if m == 1 else [m]):
                            av(*prev, k)
                    for _ in range(S1_AT[m]):
                        bb, gg, n = todo.pop(0)
                        if there(bb, 0, B):
                            s1(bb, gg, n)
                    if m == M_AT and there(nxt[0], 0, B):
                        max_to_rows(*nxt)
                    if g == 1 and m == Y_AT and there(b, 1, B):
                        project_out(b - 1)
                    if g == 0 and m in K_AT and there(b, 0, B - 2):
                        k_chunk(b + 2, K_AT[m])
                    if g == 1 and m in V_AT and there(b, 0, B - 1):
                        v_chunk(b + 1, V_AT[m])

            def batch(b):
                for g in range(GROUPS):
                    step(b, g)

            over_batches(pe, batch)
            for m in range(MT):
                av(B - 1, 1, m)
            project_out(B - 1)

            pe.wait_ge(sw_in, 16 * N_SW)
            mm(ps[:, 4, 0:128], lora[:, 0, :], lora[:, 1, :], start=True, stop=True)
            mm(ps[:, 5, 0:128], lora[:, 2, :], lora[:, 3, :], start=True, stop=True).then_inc(lora_pe, 1)
            pe.wait_ge(lora_ev, 4)
            mm(ps[:, 6, 0:128], lw[:, 0, :], lw[:, 5, :], start=True, stop=True)
            mm(ps[:, 6, 128:256], lw[:, 2, :], lw[:, 6, :], start=True, stop=True)
            mm(ps[:, 6, 256:384], sbvc[:], lw[:, 6, :], start=True, stop=True)
            mm(ps[:, 6, 384:386], lw[:, 5, :], biases[:, 2:4], start=True, stop=True).then_inc(lora_pe, 1)
            turn_tiles(1, xn1)
            pe.wait_ge(lora_ev, 8)
            for w in range(2):
                for q in range(4):
                    pe.wait_ge(ln_ev, 4 + q + 1)
                    n = 4 + 4 * w + q
                    if w:
                        pe.wait_ge(proj_ev, n - 3)
                    mm(ps[:, 4 + q, :], lw[:, 3 if w == 0 else 1, :], xnT1[:, 512 * q:512 * q + 512],
                       start=True, stop=True).then_inc(proj, 1)
            for q in range(4):
                for j in range(4):
                    m = 4 * q + j
                    last = mm(ps[:, q, 128 * j:128 * j + 128], xnT1[:, 128 * m:128 * m + 128], lw[:, 4, :],
                              start=True, stop=True)
                last.then_inc(proj, 1)
            pe.wait_ge(pads, 9)

            def scores_for_max(j):
                pe.wait_ge(b_st, j + 1)
                wait(pe, b_rows, 2 * j if isinstance(j, int) else j * 2)
                for e in range(2):
                    for p in range(PAIRS):
                        last = mm(ps[:, e, N * p:N * p + N], Q2st[0:ROWS, JP(j), e, p, :],
                                  K2st[0:ROWS, JP(j), p, N * e:N * e + N], start=True, stop=True)
                last.then_inc(b_s1, 1)

            def rows_of_max(j):
                pe.wait_ge(b_chain, j * 5 + 5)
                if not isinstance(j, int) or j > 1:
                    pe.wait_ge(b_x, j - 1)
                for e in range(2):
                    for p in range(PAIRS):
                        last = mm(ps[96:99, 2 * e + p // 4, 128 * (p % 4):128 * (p % 4) + 128],
                                  nmp2[:, JP(j), PAIRS * e + p, :], identb[:], start=True, stop=True)
                    last.then_inc(b_nm, 1)

            def JP(j):
                return j % 2 if isinstance(j, int) else JPAR[0]

            JPAR = [0]

            def shifted_scores(j):
                pe.wait_ge(b_rows, j * 2 + 2)
                wait(pe, b_exp, j)
                for e in range(2):
                    for p in range(PAIRS):
                        last = mm(ps[N * e:N * e + N, 4 + p // 4, 128 * (p % 4):128 * (p % 4) + 128],
                                  K2st[0:ROWS + 3, JP(j), p, N * e:N * e + N], Q2st[0:ROWS + 3, JP(j), e, p, :],
                                  start=True, stop=True)
                last.then_inc(b_s2, 1)

            def values(j):
                pe.wait_ge(b_exp, j + 1)
                pe.wait_ge(b_v, j + 1)
                wait_alone(pe, b_norm, j * 3)
                for e in range(2):
                    for p in range(PAIRS):
                        q = 32 * (p % 4)
                        last = mm(ps[q:q + 32, 6 + e, 128 * (p // 4):128 * (p // 4) + 128],
                                  V2st[N * e:N * e + N, JP(j), p, :], P2[N * e:N * e + N, p, :], start=True, stop=True)
                last.then_inc(b_av, 1)

            def outputs(j, more):
                pe.wait_ge(b_norm, j * 3 + 3)
                pe.wait_ge(b_rows, (j + 2) * 2 if more else 2 * TILES)
                for e in range(2):
                    for g in range(GROUPS):
                        for h in range(2):
                            last = mm(ps[N * e:N * e + N, 2, 0:C], On2[:, 2 * e + g, N * h:N * h + N], WpP[:, g, h, :],
                                      start=(g == 0 and h == 0), stop=(g == 1 and h == 1))
                last.then_inc(b_y, 1)

            pe.wait_ge(vals, 4)
            pe.wait_ge(proj_ev, 12)
            pe.wait_ge(stack_in, 16 * 2 * SLOTS)
            scores_for_max(0)
            rows_of_max(0)

            def pair(j, par, more=True):
                JPAR[0] = (par + 1) % 2
                if more:
                    scores_for_max(j + 1)
                JPAR[0] = par
                shifted_scores(j)
                JPAR[0] = (par + 1) % 2
                if more:
                    rows_of_max(j + 1)
                JPAR[0] = par
                values(j)
                outputs(j, more)

            pair(0, 0)
            with pe.Fori(0, (TILES - 2) // 2) as i:
                pair(i * 2 + 1, 1)
                pair(i * 2 + 2, 0)
            pair(TILES - 1, 1, more=False)

            turn_tiles(2, xn1)
            pe.wait_ge(ln_ev, 12)
            pe.wait_ge(fw_in, 16 * 5)
            for m in range(TILES):
                last = mm(ps[:, 4, 8 * m:8 * m + 8], xnT1[:, 128 * m:128 * m + 128], gateT[:], start=True, stop=True)
            last.then_inc(g_pe, 1)
            pe.wait_ge(g_chain, 1)

            def hidden(q, e, m):
                n = q * (EXPERTS * HT) + (HT * e + m)
                if not isinstance(n, int) or n >= 2:
                    pe.wait_ge(h_done, n - 1)
                x_q = xnT1[:, bass.ds(q * CHUNK, CHUNK)]
                mm(ps[:, m % 2, :], W1T[:, e, 128 * m:128 * m + 128], x_q, start=True, stop=True)
                mm(ps[:, 2 + m % 2, :], W3T[:, e, 128 * m:128 * m + 128], x_q, start=True, stop=True).then_inc(h_pe, 1)

            def expert_out(q, e):
                n = q * EXPERTS + e
                pe.wait_ge(h_done, n * HT + HT)
                if not isinstance(n, int) or n >= 2:
                    pe.wait_ge(y_done, n - 1)
                for k in range(CT):
                    for m in range(HT):
                        last = mm(ps[:, 5 + e % 2, 128 * k:128 * k + 128], hT[:, e % 2, m, 128 * k:128 * k + 128],
                                  W2T[:, e, m, :], start=(m == 0), stop=(m == HT - 1))
                last.then_inc(y_pe, 1)

            def chunk(q, before):
                for e in range(EXPERTS):
                    for m in range(HT):
                        hidden(q, e, m)
                        if m == 1:
                            if e:
                                expert_out(q, e - 1)
                            elif before is not None:
                                expert_out(before, EXPERTS - 1)

            chunk(0, None)
            with pe.Fori(1, CHUNKS) as q:
                chunk(q, q - 1)
            expert_out(CHUNKS - 1, EXPERTS - 1)

        @block.scalar
        def _(act):
            def deviations(k):
                act.wait_ge(ln_stat, LN_STEPS * k + 2)
                nc.scalar.activation(std[:], mv[:, :, 1], ACT.Sqrt, bias=eps[:, 0:1]).then_inc(ln_std, 1)

            def evacuate(k, xnT):
                for q in range(TILES // 4):
                    act.wait_ge(ln_tr, k * (TILES // 4) + q + 1)
                    nc.scalar.activation(xnT[:, 512 * q:512 * q + 512], ps[:, q, :], ACT.Copy).then_inc(ln_ev, 1)

            deviations(0)
            evacuate(0, xnT0)

            def k_in(b, c):
                at, w = CUTS[c]
                if c == 0 and there(b, 2, B):
                    act.wait_ge(kd_in[parity(b)], count(lambda n: 16 * NCUT * (n // 2), b))
                act.wait_ge(k_full, count(lambda n: NCUT * n + c + 1, b))
                nc.scalar.activation(Kpart[:, parity(b), 0, at:at + w], psK[:, 0:w], ACT.Identity,
                                     bias=BK).then_inc(khi_done, 1)
                wait(act, klo_done, count(lambda n: NCUT * n + c - 1, b))
                nc.scalar.activation(Krest[:, c % 2, 0:w], psK[:, 0:w], ACT.Identity, bias=BK).then_inc(kf_done, 1)

            def v_in(b, c):
                n = min(VT, MT - VT * c)
                w = 128 if c < NV - 1 else LAST_ROWS
                act.wait_ge(bank_full, count(lambda k: USE["v", k, c] + 1, b))
                nc.scalar.activation(V[0:w, parity(b), VT * c:VT * c + n, :, 0:16],
                                     psM[0:w, 0:128 * n].rearrange("p (m a k) -> p m a k", a=PAIRS, k=16),
                                     ACT.Copy).then_inc(v_done, 1)

            def exp(b, g, m):
                u = units(b, g)
                act.wait_ge(s2_done, u(MT, m + 1))
                wait(act, av_done, u(MT, m + 1 - MT))
                nc.scalar.activation(P[:, m, :], psS2[:, (m + g) % 3, :], ACT.Exp).then_inc(exp_done, 1)

            def rows(b, g):
                act.wait_ge(bank_full, count(lambda n: USE["m", n, g] + 1, b))
                act.wait_ge(qst_done, units(b, g)(1, 1))
                nc.scalar.activation(Qst[96:99, parity(b), g, :, :], psM[96:99, :].rearrange("p (j q) -> p j q", j=GP),
                                     ACT.Copy).then_inc(max_rows, 1)

            act.wait_ge(w_in, 16 * N_W)
            for b in range(2):
                for c in range(NCUT):
                    k_in(b, c)
            act.wait_ge(pads, 6)
            for c in range(NV):
                v_in(0, c)
            rows(0, 0)
            act.wait_ge(qst_in, 16 * SLOTS)

            def batch(b):
                for g in range(GROUPS):
                    for m in range(MT):
                        exp(b, g, m)
                        if g == 0 and m in K_AT and there(b, 0, B - 2):
                            k_in(b + 2, K_AT[m])
                        if g == 1 and m in V_AT and there(b, 0, B - 1):
                            v_in(b + 1, V_AT[m])
                        nxt = neighbour(b, g, 1)
                        if m == M_AT + 1 and there(nxt[0], 0, B):
                            rows(*nxt)

            over_batches(act, batch)

            deviations(1)
            evacuate(1, xnT1)

            def rows_in(j, par):
                for e in range(2):
                    act.wait_ge(b_nm, j * 2 + e + 1)
                    act.wait_ge(b_st, j + 1)
                    nc.scalar.activation(Q2st[96:99, par, e, :, :],
                                         ps[96:99, 2 * e:2 * e + 2, :].rearrange("p a (b q) -> p (a b) q", b=4),
                                         ACT.Copy).then_inc(b_rows, 1)

            def pair(j, par, more=True):
                act.wait_ge(b_s2, j + 1)
                wait(act, b_av, j)
                v = V2[:, j, :] if isinstance(j, int) else V2[:, bass.ds(j, 1), :].rearrange("p o c -> p (o c)")
                nc.scalar.activation(V2st[:, par, :, 0:16], v.rearrange("p (a b) -> p a b", b=16),
                                     ACT.Copy).then_inc(b_v, 1)
                nc.scalar.activation(P2[:].rearrange("p a b -> p (a b)"),
                                     ps[:, 4:6, :].rearrange("p a b -> p (a b)"), ACT.Exp).then_inc(b_exp, 1)
                if more:
                    rows_in(j + 1, 1 - par)

            act.wait_ge(vals, 4)
            act.wait_ge(pads, 9)
            rows_in(0, 0)
            pair(0, 0)
            with act.Fori(0, (TILES - 2) // 2) as i:
                pair(i * 2 + 1, 1)
                pair(i * 2 + 2, 0)
            pair(TILES - 1, 1, more=False)

            deviations(2)
            evacuate(2, xnT1)
            act.wait_ge(g_chain, 4)
            nc.scalar.activation(tw[:, 1, :], tw[:, 0, :], ACT.Exp).then_inc(g_exp, 1)

            def silu(q, e, m):
                n = q * (EXPERTS * HT) + (HT * e + m)
                act.wait_ge(h_pe, n + 1)
                if not isinstance(n, int) or n >= 2:
                    act.wait_ge(h_done, n - 1)
                nc.scalar.activation(sil[:, m % 2, :], ps[:, m % 2, :], ACT.Silu).then_inc(h_sil, 1)

            def chunk(q):
                for e in range(EXPERTS):
                    for m in range(HT):
                        silu(q, e, m)

            chunk(0)
            with act.Fori(1, CHUNKS) as q:
                chunk(q)

        @block.vector
        def _(dve):
            v = nc.vector
            v.memset(eps[:], EPS)
            dve.wait_ge(load, 16 * N_LOAD)
            v.tensor_copy(identb[:], ident[:]).then_inc(made, 1)

            def normalise(k, xn):
                s0 = LN_STEPS * k
                for m in range(TILES):
                    last = v.bn_stats(stats[:, m, :], x_all[:, m, :])
                last.then_inc(ln_stat, 1)
                dve.wait_ge(ln_stat, s0 + 1)
                for m in range(TILES):
                    last = v.bn_aggr(mv[:, m, :], stats[:, m, :])
                last.then_inc(ln_stat, 1)
                dve.wait_ge(ln_std, k + 1)
                v.reciprocal(rstd[:], std[:]).then_inc(ln_stat, 1)
                dve.wait_ge(ln_stat, s0 + 3)
                for m in range(TILES):
                    last = v.tensor_scalar(xn[:, m, :], x_all[:, m, :], mv[:, m, 0:1], rstd[:, m:m + 1],
                                           ALU.subtract, ALU.mult)
                last.then_inc(ln_stat, 1)

            def project_and_split(n0, s0, bias, scale, qf, parts):
                for q in range(4):
                    dve.wait_ge(proj, n0 + q + 1)
                    v.tensor_scalar(qf[:, 512 * q:512 * q + 512], ps[:, 4 + q, :], bias, scale,
                                    ALU.add, ALU.mult).then_inc(proj_ev, 1)
                dve.wait_ge(proj_ev, n0 + 4)
                v.tensor_copy(parts[:, 0, :], qf).then_inc(split, 1)
                dve.wait_ge(split, s0 + 1)
                v.tensor_tensor(qf, qf, parts[:, 0, :], ALU.subtract).then_inc(split, 1)
                dve.wait_ge(split, s0 + 2)
                v.tensor_copy(parts[:, 1, :], qf).then_inc(split, 1)
                dve.wait_ge(split, s0 + 3)
                v.tensor_tensor(parts[:, 2, :], qf, parts[:, 1, :], ALU.subtract).then_inc(split, 1)

            normalise(0, xn0)
            project_and_split(0, 0, BQ, SCALE, qf0, qparts0)

            def k_mid(b, c):
                at, w = CUTS[c]
                dve.wait_ge(krest_done, count(lambda n: NCUT * n + c + 1, b))
                v.tensor_copy(Kpart[:, parity(b), 1, at:at + w], Krest[:, c % 2, 0:w]).then_inc(kmid_done, 1)

            def query_stack(b, g):
                u = units(b, g)
                wait(dve, s2_done, u(MT, -3 * MT))
                for h in range(2):
                    last = v.tensor_scalar(Qst[0:ROWS, parity(b), g, :, N * h:N * h + N],
                                           Qall[0:ROWS, GP * g:GP * g + GP, bass.ds(value(b) * N, N)],
                                           head_rows[0:ROWS, h:h + 1], None, ALU.mult)
                last.then_inc(qst_done, 1)

            def chunk_max(b, g, n):
                j, c = divmod(n, NCUT)
                dve.wait_ge(s1_done, units(b, g)(UC, n + 1))
                v.tensor_reduce(mxc[:, g, j, c:c + 1], psS1[:, n % 2, 0:CUTS[c][1]], AX.X, ALU.max)\
                 .then_inc(max_done, 1)

            def split_max(b, g):
                u = units(b, g)
                dve.wait_ge(max_done, u(UC, UC))
                v.tensor_reduce(nmf[:, g, :], mxc[:, g, :, :], AX.X, ALU.max, negate=True).then_inc(nm_chain, 1)
                dve.wait_ge(nm_chain, u(5, 1))
                v.tensor_copy(nmp[:, g, :, 0], nmf[:, g, :]).then_inc(nm_chain, 1)
                dve.wait_ge(nm_chain, u(5, 2))
                v.tensor_tensor(nmf[:, g, :], nmf[:, g, :], nmp[:, g, :, 0], ALU.subtract).then_inc(nm_chain, 1)
                dve.wait_ge(nm_chain, u(5, 3))
                v.tensor_copy(nmp[:, g, :, 1], nmf[:, g, :]).then_inc(nm_chain, 1)
                dve.wait_ge(nm_chain, u(5, 4))
                v.tensor_tensor(nmp[:, g, :, 2], nmf[:, g, :], nmp[:, g, :, 1], ALU.subtract).then_inc(nm_chain, 1)

            def read_out(b, g):
                dve.wait_ge(av_done, units(b, g)(MT, MT))
                v.tensor_copy(O[:, g, :], psO[:, 0:128]).then_inc(o_read, 1)

            def sums_up(b, g):
                u = units(b, g)
                wait_alone(dve, o_read, u(1, 1))
                v.stream_shuffle(den[:, g, :], O[:, g, :], SUM_ROWS).then_inc(den_done, 1)
                dve.wait_ge(den_done, u(2, 1))
                v.reciprocal(den[:, g, :], den[:, g, :]).then_inc(den_done, 1)

            def residual(b):
                dve.wait_ge(bank_full, count(lambda n: USE["y", n, 0] + 1, b))
                r = N * parity(b)
                m = bass.ds(value(b - parity(b)) // 2, 1) if isinstance(b, int) else bass.ds(b.i + b.off // 2, 1)
                x = x_all[r:r + N, m, :].rearrange("p o c -> p (o c)")
                v.tensor_tensor(x, psM[r:r + N, 0:C], x, ALU.add).then_inc(x1_done, 1)

            dve.wait_ge(bo_pe, 1)
            v.tensor_copy(bo[:], ps[:, 4, 0:128]).then_inc(bo_done, 1)
            dve.wait_ge(bo_done, 1)
            v.tensor_tensor(x_all[:], x_all[:], bo[:].unsqueeze(1).broadcast_to((128, TILES, C)), ALU.add)\
             .then_inc(bo_done, 1)
            dve.wait_ge(bo_done, 2)
            for b in range(2):
                for c in range(NCUT):
                    k_mid(b, c)
            dve.wait_ge(qst_in, 16 * SLOTS)
            for g in range(GROUPS):
                query_stack(0, g)
            for n in range(UC):
                chunk_max(0, 0, n)
            split_max(0, 0)
            for n in range(S1_AHEAD):
                chunk_max(0, 1, n)

            def step(b, g):
                nxt, old = neighbour(b, g, 1), neighbour(b, g, -2)
                if there(old[0], 0, B):
                    read_out(*old)
                todo = s1_chunks(b, g)
                for m in range(MT):
                    for _ in range(S1_AT[m]):
                        bb, gg, n = todo.pop(0)
                        if there(bb, 0, B):
                            chunk_max(bb, gg, n)
                        if n == UC - 1 and there(bb, 0, B):
                            split_max(bb, gg)
                    if m == 1 and there(old[0], 0, B):
                        sums_up(*old)
                    if m == QST_AT and there(b, 0, B - 1):
                        query_stack(b + 1, g)
                    if g == 0 and m in KMID_AT and there(b, 0, B - 2):
                        k_mid(b + 2, KMID_AT[m])
                    if g == 1 and m == Y_AT + 1 and there(b, 1, B):
                        residual(b - 1)

            def batch(b):
                for g in range(GROUPS):
                    step(b, g)

            over_batches(dve, batch)
            for g in range(GROUPS):
                read_out(B - 1, g)
                sums_up(B - 1, g)
            residual(B - 1)

            dve.wait_ge(x1_done, B)
            normalise(1, xn1)
            dve.wait_ge(sw_in, 16 * N_SW)
            dve.wait_ge(lora_pe, 1)
            for n in range(2):
                v.tensor_tensor(lw[:, 8 + n, :], ps[:, 4 + n, 0:128], lw[:, 7, :], ALU.mult).then_inc(lora_ev, 1)
            dve.wait_ge(lora_ev, 2)
            for n in range(2):
                v.scalar_tensor_tensor(lw[:, 5 + n, :], lw[:, 8 + n, :], LORA, ident[:],
                                       ALU.mult, ALU.add).then_inc(lora_ev, 1)
            dve.wait_ge(lora_pe, 2)
            v.tensor_copy(lw[:, 3, :], ps[:, 6, 0:128]).then_inc(lora_ev, 1)
            v.tensor_copy(lw[:, 4, :], ps[:, 6, 128:256]).then_inc(lora_ev, 1)
            v.tensor_copy(bv2[:], ps[:, 6, 256:384]).then_inc(lora_ev, 1)
            v.tensor_copy(SBQ2, ps[:, 6, 384:385]).then_inc(lora_ev, 1)
            dve.wait_ge(lora_ev, 8)
            project_and_split(4, 4, SBQ2, SCALE, qf1[:], qparts1)
            for q in range(4):
                dve.wait_ge(proj, 12 + q + 1)
                for j in range(4):
                    last = v.tensor_tensor(V2[:, 4 * q + j, :], ps[:, q, 128 * j:128 * j + 128], bv2[:], ALU.add)
                last.then_inc(vals, 1)
            dve.wait_ge(stack_in, 16 * SLOTS)
            dve.wait_ge(split, 8)
            project_and_split(8, 8, SBK, 1.0, qf1[:], qparts1)
            dve.wait_ge(stack_in, 16 * 2 * SLOTS)
            dve.wait_ge(pads, 9)

            def stacks(j, par):
                if isinstance(j, int):
                    if j >= 2:
                        dve.wait_ge(b_s2, j - 1)
                else:
                    dve.wait_ge(b_s2, j - 1)
                for e in range(2):
                    for h in range(2):
                        v.tensor_scalar(Q2st[0:ROWS, par, e, :, N * h:N * h + N],
                                        Qall[0:ROWS, :, bass.ds(j * 128 + N * e, N)],
                                        head_rows[0:ROWS, h:h + 1], None, ALU.mult)
                v.tensor_copy(K2st[0:ROWS, par, :, :], Kall[0:ROWS, :, bass.ds(j * 128, 128)]).then_inc(b_st, 1)

            def maxima(j, par):
                dve.wait_ge(b_s1, j + 1)
                v.tensor_reduce(nmf2[:, par, :], ps[:, 0:2, :].rearrange("p e (a m) -> p (e a) m", m=N), AX.X,
                                ALU.max, negate=True).then_inc(b_chain, 1)
                dve.wait_ge(b_chain, j * 5 + 1)
                v.tensor_copy(nmp2[:, par, :, 0], nmf2[:, par, :]).then_inc(b_chain, 1)
                dve.wait_ge(b_chain, j * 5 + 2)
                v.tensor_tensor(nmf2[:, par, :], nmf2[:, par, :], nmp2[:, par, :, 0], ALU.subtract).then_inc(b_chain, 1)
                dve.wait_ge(b_chain, j * 5 + 3)
                v.tensor_copy(nmp2[:, par, :, 1], nmf2[:, par, :]).then_inc(b_chain, 1)
                dve.wait_ge(b_chain, j * 5 + 4)
                v.tensor_tensor(nmp2[:, par, :, 2], nmf2[:, par, :], nmp2[:, par, :, 1], ALU.subtract)\
                 .then_inc(b_chain, 1)

            def pair(j, par, more=True):
                if more:
                    stacks(j + 1, 1 - par)
                    maxima(j + 1, 1 - par)
                wait_alone(dve, b_av, j + 1)
                o = ps[:, 6:8, 0:2 * 128]
                v.stream_shuffle(den2[:].rearrange("p (e g) b -> p e (g b)", e=2), o, SUM_ROWS).then_inc(b_norm, 1)
                dve.wait_ge(b_norm, j * 3 + 1)
                v.reciprocal(rden2[:].rearrange("p a b -> p (a b)"), den2[:].rearrange("p a b -> p (a b)"))\
                 .then_inc(b_norm, 1)
                dve.wait_ge(b_norm, j * 3 + 2)
                v.tensor_tensor(On2[:].rearrange("p (e g) b -> p e (g b)", e=2), o,
                                rden2[:].rearrange("p (e g) b -> p e (g b)", e=2), ALU.mult).then_inc(b_norm, 1)
                dve.wait_ge(b_y, j + 1)
                v.tensor_tensor(ytmp[:], ps[:, 2, 0:C], bp[:], ALU.add).then_inc(b_xa, 1)
                dve.wait_ge(b_xa, j + 1)
                x = x_all[:, bass.ds(j, 1), :].rearrange("p o c -> p (o c)")
                v.tensor_tensor(x, x, ytmp[:], ALU.add).then_inc(b_x, 1)

            stacks(0, 0)
            maxima(0, 0)
            pair(0, 0)
            with dve.Fori(0, (TILES - 2) // 2) as i:
                pair(i * 2 + 1, 1)
                pair(i * 2 + 2, 0)
            pair(TILES - 1, 1, more=False)

            dve.wait_ge(b_x, TILES)
            normalise(2, xn1)
            dve.wait_ge(fw_in, 16 * 5)
            dve.wait_ge(g_pe, 1)
            v.tensor_copy(gs[:].rearrange("p a b -> p (a b)"), ps[:, 4, 0:8 * TILES]).then_inc(g_chain, 1)
            dve.wait_ge(g_chain, 1)
            for m in range(TILES):
                last = v.max(top[:, m, :], gs[:, m, :])
            last.then_inc(g_chain, 1)
            dve.wait_ge(g_chain, 2)
            for m in range(TILES):
                last = v.max_index(topi[:, m, :], top[:, m, :], gs[:, m, :])
            last.then_inc(g_chain, 1)
            dve.wait_ge(g_chain, 3)
            v.tensor_copy(topf[:], topi[:])
            v.tensor_tensor(tw[:, 0, :], top[:, :, 1], top[:, :, 0], ALU.subtract).then_inc(g_chain, 1)
            dve.wait_ge(g_exp, 1)
            v.tensor_scalar(tw[:, 2, :], tw[:, 1, :], 1.0, None, ALU.add).then_inc(g_chain, 1)
            dve.wait_ge(g_chain, 5)
            v.reciprocal(tw[:, 2, :], tw[:, 2, :]).then_inc(g_chain, 1)
            dve.wait_ge(g_chain, 6)
            v.tensor_tensor(tw[:, 3, :], tw[:, 1, :], tw[:, 2, :], ALU.mult).then_inc(g_chain, 1)
            dve.wait_ge(g_chain, 7)
            for m in range(TILES):
                v.tensor_scalar(comb[:, m, :], iota[:], topf[:, m, 0:1], tw[:, 2, m:m + 1], ALU.is_equal, ALU.mult)
                last = v.tensor_scalar(comb2[:, m, :], iota[:], topf[:, m, 1:2], tw[:, 3, m:m + 1],
                                       ALU.is_equal, ALU.mult)
            last.then_inc(g_chain, 1)
            dve.wait_ge(g_chain, 8)
            v.tensor_tensor(comb[:], comb[:], comb2[:], ALU.add).then_inc(g_chain, 1)
            dve.wait_ge(g_chain, 9)

            def hidden(q, e, m):
                n = q * (EXPERTS * HT) + (HT * e + m)
                dve.wait_ge(h_sil, n + 1)
                if not isinstance(n, int) or n >= 2 * HT:
                    dve.wait_ge(y_pe, q * EXPERTS + e - 1)
                v.tensor_tensor(hT[:, e % 2, m, :], ps[:, 2 + m % 2, :], sil[:, m % 2, :], ALU.mult).then_inc(h_done, 1)

            def add_expert(q, e):
                n = q * EXPERTS + e
                dve.wait_ge(y_pe, n + 1)
                if isinstance(n, int):
                    wait(dve, y_done, n)
                else:
                    dve.wait_ge(y_done, n)
                for k in range(CT):
                    w = comb[:, bass.ds(q * CT + k, 1), e:e + 1].rearrange("p o e -> p (o e)")
                    before = x_all[:, bass.ds(q * CT + k, 1), :].rearrange("p o c -> p (o c)") if e == 0 else \
                        acc[:, (e + 1) % 2, k, :]
                    last = v.scalar_tensor_tensor(acc[:, e % 2, k, :], ps[:, 5 + e % 2, 128 * k:128 * k + 128], w,
                                                  before, ALU.mult, ALU.add)
                last.then_inc(y_done, 1)

            def finish(q, par):
                add_expert(q, EXPERTS - 1)
                dve.wait_ge(y_done, q * EXPERTS + EXPERTS)
                wait(dve, o_out[par], 16 * (q // 2))
                v.tensor_copy(out_t[:, par], acc[:, (EXPERTS - 1) % 2]).then_inc(o_done, 1)

            def chunk_with(q, before, par):
                for e in range(EXPERTS):
                    for m in range(HT):
                        hidden(q, e, m)
                        if m == 1:
                            if e:
                                add_expert(q, e - 1)
                            elif before is not None:
                                finish(before, par)

            for q in range(CHUNKS):
                chunk_with(q, q - 1 if q else None, (q - 1) % 2)
            finish(CHUNKS - 1, (CHUNKS - 1) % 2)


def kernel(**inputs):
    import concourse.bacc as bacc
    from concourse.bass_utils import run_bass_kernel_spmd as run

    g = {k: np.asarray(v) for k, v in inputs.items()}
    xa, at, ff = "L0_xattn_", "L0_attn_", "L0_ffn_"

    def by_pair(w):
        o = np.zeros((GP, 32, GROUPS, 2, C), w.dtype)
        w = w.reshape(GROUPS, GP, 2, D, C)
        for h in range(2):
            o[:, D * h:D * h + D, :, h, :] = w[:, :, h].transpose(1, 2, 0, 3)
        return o.reshape(128, GROUPS, 2, C)

    wqkv, bqkv = g[at + "w_qkv"], g[at + "b_qkv"].reshape(3, C, 1)
    rows = np.arange(128)
    f = np.float32
    arrays = {
        "x": g["x"].reshape(T, C), "ctxT": g["ctx_1024"].transpose(0, 2, 1),
        "WqT": g[xa + "Wq"].T, "WkT": g[xa + "Wk"].T, "WvT": g[xa + "Wv"].T, "WoP": by_pair(g[xa + "Wo"].T),
        "bq": g[xa + "bq"].reshape(C, 1), "bk": g[xa + "bk"].reshape(C, 1), "bv": np.tile(g[xa + "bv"].reshape(C, 1), (1, 128)), "WoT": g[xa + "Wo"].T,
        "wqT": wqkv[:, 0:C].T, "wk": wqkv[:, C:2 * C], "wvT": wqkv[:, 2 * C:].T,
        "sbq": bqkv[0], "sbk": bqkv[1], "sbv": np.tile(bqkv[2], (1, 128)),
        "aqT": np.tile(g[at + "a_q"].T, (1, H)), "bbq": np.tile(g[at + "b_q"], (1, H)),
        "avT": np.tile(g[at + "a_v"].T, (1, H)), "bbv": np.tile(g[at + "b_v"], (1, H)),
        "WpP": by_pair(g[at + "w_proj"]), "bp": g[at + "b_proj"].reshape(1, C),
        "gateT": g[ff + "gate_w"].T, "W1T": g[ff + "w1"].transpose(2, 0, 1), "W3T": g[ff + "w3"].transpose(2, 0, 1),
        "W2T": g[ff + "w2"].transpose(2, 0, 1).reshape(HT, 128, EXPERTS, C).transpose(1, 2, 0, 3),
        "ident": np.eye(128, dtype=f), "head_rows": (rows[:, None] // D % 2 == np.arange(2)).astype(f),
        "head_block": (rows[:, None] // D == rows // D).astype(f),
        "iota": np.tile(np.arange(EXPERTS, dtype=f), (128, 1)),
    }
    nc = bacc.Bacc("TRN2", target_bir_lowering=False, num_devices=1)
    t = {}
    for name, shape in INS.items():
        arrays[name] = np.ascontiguousarray(arrays[name])
        assert arrays[name].shape == shape, name
        t[name] = nc.dram_tensor("in_" + name, shape, F32, kind="ExternalInput").ap()
    out = nc.dram_tensor("out", (T, C), F32, kind="ExternalOutput").ap()
    perceiver(nc, t, out)
    r = run(nc, [{"in_" + n: a for n, a in arrays.items()}], core_ids=[0])
    return r.results[0]["out"].reshape(B, N, C)
```

```python
from contextlib import ExitStack

import concourse.bass as bass
from concourse import mybir
import numpy as np

F32 = mybir.dt.float32
BF16 = mybir.dt.bfloat16
U32 = mybir.dt.uint32
ALU = mybir.AluOpType
ACT = mybir.ActivationFunctionType
AX = mybir.AxisListType

B, N, C = 32, 64, 128
M = 1601
H, D = 16, 8
T = B * N
TILES = T // 128
PAIRS = H // 2
GROUPS = 2
GP = PAIRS // GROUPS
MT = -(-M // 128)
MPAD = MT * 128
LAST_ROWS = M - 128 * (MT - 1)
K_PART = [0, 0, 0, 1, 1, 2]
Q_PART = [0, 1, 2, 0, 1, 0]
SLOTS = len(K_PART)
ROWS = SLOTS * 2 * D
CUTS = [(0, 402), (402, 400), (802, 400), (1202, 399)]
NCUT = len(CUTS)
UC = GP * NCUT
S1_AT = [2, 1, 1, 1, 1, 1, 1, 2, 1, 1, 1, 1, 2]
S1_AHEAD = UC // 2
M_AT = 9
K_AT = {1: 0, 4: 1, 7: 2, 11: 3}
KMID_AT = {(0, 4): 0, (0, 7): 1, (0, 10): 2, (1, 1): 3}
V_AT = {0: 0, 2: 1, 4: 2, 6: 3}
S1_BANK = [0, 1, 2] * (UC // 3) + [1]
S1_BACK = [next(k for k in range(1, UC) if S1_BANK[n - k] == S1_BANK[n]) for n in range(UC)]
QST_AT = 3
Y_AT = 11
S2_BACK = [[2, 2, 5] + [3] * (MT - 3), [3] * MT]
VT = 4
NV = -(-MT // VT)
EXPERTS, HID, TOPK = 8, 512, 2
HT = HID // 128
CHUNK = 512
CHUNKS = T // CHUNK
CT = CHUNK // 128
EPS = 1e-5
SCALE = float(D) ** -0.5
LORA = 2.0
R = 16
LN_STEPS = 3 + TILES // 4
QUARTERS = TILES // 4
QW = T // QUARTERS
VS = 4 * D
SUM_ROWS = [16 + n % 16 for n in range(32)]
N_SW = 15
FIRST, LAST = 1, B // 2 - 3

INS = {
    "x": (T, C), "ctxT": (B, C, M), "WqT": (C, C), "WkT": (C, C), "WvT": (C, C), "WoP": (128, GROUPS, 2, C), "WoT": (C, C),
    "bq": (C, 1), "bk": (C, 1), "bv": (C, 128), "wqT": (C, C), "wk": (C, C), "wvT": (C, C),
    "sbq": (C, 1), "sbk": (C, 1), "sbv": (C, 128), "aqT": (R, C), "bbq": (R, C), "avT": (R, C), "bbv": (R, C),
    "Wp": (C, C), "WpE": (128, GROUPS, 2, 2, C), "batch_ones": (128, VS), "bp": (1, C), "gateT": (C, EXPERTS), "W1T": (C, EXPERTS, HID),
    "W3T": (C, EXPERTS, HID), "W2T": (128, EXPERTS, HT, C),
    "ident": (128, 128), "head_rows": (128, 2), "head_block": (128, 128), "iota": (128, EXPERTS),
}


class Batch:

    def __init__(self, i, off):
        self.i, self.off = i, off

    def __add__(self, k):
        return Batch(self.i, self.off + k)

    def __sub__(self, k):
        return Batch(self.i, self.off - k)


def parity(b):
    return (b if isinstance(b, int) else b.off) % 2


def value(b):
    return b if isinstance(b, int) else b.i * 2 + b.off


def count(f, b):
    if isinstance(b, int):
        return f(b)
    slope = f(b.off + 2 * FIRST + 2) - f(b.off + 2 * FIRST)
    return b.i * slope + (f(b.off + 2 * FIRST) - slope * FIRST)


def uses():
    out = [("k", b, c) for b in range(2) for c in range(NCUT)] + [("v", 0, c) for c in range(NV)] + [("m", 0, 0)]
    for b in range(B):
        for g in range(GROUPS):
            for s in range(MT):
                if g == 0 and s in K_AT and b + 2 < B:
                    out.append(("k", b + 2, K_AT[s]))
                if s == M_AT and (g == 0 or b + 1 < B):
                    out.append(("m", b + g, 1 - g))
                if g == 1 and s == Y_AT and b:
                    out.append(("y", b - 1, 0))
                if g == 1 and s in V_AT and b + 1 < B:
                    out.append(("v", b + 1, V_AT[s]))
    out.append(("y", B - 1, 0))
    return out


ORDER = uses()
USE = {u: n for n, u in enumerate(ORDER)}


def perceiver(nc, t, out):
    ctx = ExitStack()
    scope = ExitStack()

    def sb(name, shape, dt=F32, where=ctx):
        return where.enter_context(nc.sbuf_tensor(name, shape, dt))

    def sem(name):
        return ctx.enter_context(nc.semaphore(name))

    def wait(eng, s, v):
        if not isinstance(v, int) or v > 0:
            eng.wait_ge(s, v)

    with ctx:
        x_all = sb("x_all", [128, TILES, C])
        ident = sb("ident_sb", [128, 128])
        identb = sb("identb", [128, 128], BF16)
        head_rows = sb("head_rows_sb", [128, 2])
        eps = sb("eps", [128, 1])
        stats = sb("stats", [128, TILES, 6])
        mv = sb("mv", [128, TILES, 2])
        std = sb("std", [128, TILES])
        rstd = sb("rstd", [128, TILES])
        biases = sb("biases", [128, 8])
        BQ, BK, SBQ, SBK, SBV, SBQ2 = (biases[:, n:n + 1] for n in range(6))
        WqT, WkT, WvT = (sb(n, [128, 128]) for n in ("WqT_sb", "WkT_sb", "WvT_sb"))
        WoP = sb("WoP_sb", [128, GROUPS, 2, C])
        bo = sb("bo", [128, C])
        Qall = sb("Qall", [128, PAIRS, T], BF16)

        Kst = sb("Kst", [128, 2, PAIRS, MPAD], BF16, scope)
        Kpart = sb("Kpart", [128, 2, 3, M], BF16, scope)
        Krest = sb("Krest", [128, 2, CUTS[0][1]], F32, scope)
        V = sb("V", [128, 2, MT, PAIRS, 32], F32, scope)
        P = sb("P", [128, MT + 1, 512], F32, scope)
        ctxT = sb("ctxT_sb", [128, 2, M], F32, scope)
        Qst = sb("Qst", [128, 2, GROUPS, GP, 128], BF16, scope)
        mxc = sb("mxc", [128, 2, GP, NCUT], F32, scope)
        nmf = sb("nmf", [128, 2, GP], F32, scope)
        nmp = sb("nmp", [128, 2, GP, 3], BF16, scope)
        den = sb("den", [128, 2, 128], F32, scope)
        O = sb("O", [128, 2, 128], F32, scope)
        WoT = sb("WoT_sb", [128, 128], F32, scope)
        bvc = sb("bvc", [128, 128], F32, scope)
        On = sb("On", [128, 2, 128], F32, scope)
        xnT0 = P[:, 0:4, :].rearrange("p a b -> p (a b)")
        qf0 = P[:, 4:8, :].rearrange("p a b -> p (a b)")
        qparts0 = P[:, 8:14, :].rearrange("p a b -> p (a b)").bitcast(BF16).rearrange("p (k t) -> p k t", k=3)
        xn0 = V[:, 0, 0:8, :, :].rearrange("p a b c -> p (a b c)").rearrange("p (t c) -> p t c", c=C)
        scope.close()

        W1T = sb("W1T_sb", [128, EXPERTS, HID])
        W3T = sb("W3T_sb", [128, EXPERTS, HID])
        W2T = sb("W2T_sb", [128, EXPERTS, HT, C])
        gateT = sb("gateT_sb", [128, EXPERTS])
        iota = sb("iota_sb", [128, EXPERTS])
        xn1 = sb("xn1", [128, TILES, C])
        xnT1 = sb("xnT1", [128, T])
        scope2 = ExitStack()
        Kall = sb("Kall", [128, PAIRS, T], BF16, scope2)
        qk = sb("qk", [128, 2, 2, QW], F32, scope2)
        qkparts = sb("qkparts", [128, 2, 2, 3, QW], BF16, scope2)
        Vall = sb("Vall", [128, TILES, PAIRS, VS], F32, scope2)
        V2st = sb("V2st", [128, 2, PAIRS, VS], F32, scope2)
        P2 = xn1[:].rearrange("p (b a) q -> p b a q", b=2)
        K2st = sb("K2st", [128, 2, PAIRS, 128], BF16, scope2)
        Q2st = sb("Q2st", [128, 2, 2, PAIRS, 128], BF16, scope2)
        lw = sb("lw", [128, 10, 128], F32, scope2)
        lora = sb("lora", [R, 4, C], F32, scope2)
        sbvc = sb("sbvc", [128, 128], F32, scope2)
        bv2 = sb("bv2", [128, C], F32, scope2)
        bp = sb("bp_sb", [128, C], F32, scope2)
        Wp = sb("Wp_sb", [128, C], F32, scope2)
        WpE = sb("WpE_sb", [128, GROUPS, 2, 2, C], F32, scope2)
        batch_ones = sb("batch_ones_sb", [128, VS], F32, scope2)
        bo2 = sb("bo2", [128, C], F32, scope2)
        nmf2 = sb("nmf2", [128, 2, 16], F32, scope2)
        nmp2 = sb("nmp2", [128, 2, 16, 3], BF16, scope2)
        rden2 = qk[:, 0, 0, 0:GROUPS * 128]
        On2 = sb("On2", [128, 2, GROUPS, 128], F32, scope2)
        scope2.close()
        gs = sb("gs", [128, TILES, 8])
        top = sb("top", [128, TILES, 8])
        topi = sb("topi", [128, TILES, 8], U32)
        topf = sb("topf", [128, TILES, 8])
        tw = sb("tw", [128, 4, TILES])
        comb = sb("comb", [128, TILES, EXPERTS])
        comb2 = sb("comb2", [128, TILES, EXPERTS])
        sil = sb("sil", [128, 2, CHUNK])
        hT = sb("hT", [128, 2, HT, CHUNK])
        acc = sb("acc", [128, 2, CT, C])
        out_t = sb("out_t", [128, 2, CT, C])

        ps = ctx.enter_context(nc.psum_tensor("ps", [128, 8, 512], F32))
        psS1 = ps[:, 0:3, :]
        psS2 = ps[:, 3:6, :]
        psO = ps[:, 6, :]
        psM = ps[:, 7, :]

        load = sem("load")
        w_in = sem("w_in")
        sw_in = sem("sw_in")
        fw_in = sem("fw_in")
        made = sem("made")
        pads = sem("pads")
        ctx_in = [sem(f"ctx_in{n}") for n in range(2)]
        kst_in = [[sem(f"kst_in{n}{g}") for g in range(GROUPS)] for n in range(2)]
        qst_in = sem("qst_in")
        s1_done = sem("s1_done")
        s2_done = sem("s2_done")
        av_done = sem("av_done")
        bank_full = sem("bank_full")
        exp_done = sem("exp_done")
        kf_done = sem("kf_done")
        khi_done = sem("khi_done")
        max_rows = sem("max_rows")
        max_done = sem("max_done")
        nm_chain = sem("nm_chain")
        o_read = sem("o_read")
        den_done = sem("den_done")
        norm_done = sem("norm_done")
        qst_done = sem("qst_done")
        krest_done = sem("krest_done")
        kmid_done = sem("kmid_done")
        klo_done = sem("klo_done")
        kd_in = [sem(f"kd_in{n}") for n in range(2)]
        qd_in = sem("qd_in")
        bo_pe = sem("bo_pe")
        bo_done = sem("bo_done")
        v_done = sem("v_done")
        x1_done = sem("x1_done")
        ln_stat = sem("ln_stat")
        ln_std = sem("ln_std")
        ln_tr = sem("ln_tr")
        ln_ev = sem("ln_ev")
        proj = sem("proj")
        proj_ev = sem("proj_ev")
        split = sem("split")
        p_full = sem("p_full")
        hi_done = sem("hi_done")
        f_done = sem("f_done")
        parts_done = sem("parts_done")
        sd_in = [sem(f"sd_in{n}") for n in range(2)]
        stack_in = sem("stack_in")
        lora_pe = sem("lora_pe")
        lora_ev = sem("lora_ev")
        b_st = sem("b_st")
        b_kst = sem("b_kst")
        b_s1 = sem("b_s1")
        b_chain = sem("b_chain")
        b_nm = sem("b_nm")
        b_rows = sem("b_rows")
        b_s2 = sem("b_s2")
        b_exp = sem("b_exp")
        b_av = sem("b_av")
        b_norm = sem("b_norm")
        b_v = sem("b_v")
        b_y = sem("b_y")
        vals = sem("vals")
        x_b = sem("x_b")
        b_x = sem("b_x")
        g_pe = sem("g_pe")
        g_chain = sem("g_chain")
        g_exp = sem("g_exp")
        h_pe = sem("h_pe")
        h_sil = sem("h_sil")
        h_done = sem("h_done")
        y_pe = sem("y_pe")
        y_done = sem("y_done")
        o_done = sem("o_done")
        o_out = [sem(f"o_out{n}") for n in range(2)]

        def wait_alone(eng, s, v):
            v = v if isinstance(v, int) else eng.snap(eng.to_reg(v))
            eng.wait_ge(load, 16)
            wait(eng, s, v)

        N_LOAD, N_W = 4, 7
        kd = nc.dram_tensor("k_parts", (2, 3, 128, M), BF16, kind="Internal").ap()
        sd = nc.dram_tensor("self_parts", (2, 3, 128, T), BF16, kind="Internal").ap()
        qd = nc.dram_tensor("q_parts", (3, 128, T), BF16, kind="Internal").ap()
        block = ctx.enter_context(nc.Block())

        def over_batches(eng, body):
            for b in range(2 * FIRST):
                body(b)
            with eng.Fori(FIRST, LAST + 1) as i:
                for off in range(2):
                    body(Batch(i, off))
            for b in range(2 * LAST + 2, B):
                body(b)

        def there(b, lo, hi):
            return lo <= b < hi if isinstance(b, int) else True

        def units(b, g):
            return lambda k, add: count(lambda n: k * (2 * n + g) + add, b)

        def neighbour(b, g, k):
            n = g + k
            return b + n // 2, n % 2

        def exists(j):
            return not isinstance(j, int) or 0 <= j < TILES

        def over_pairs(eng, body):
            reads_stacks = eng in (nc.vector, nc.gpsimd)
            body(0, 0)
            with eng.Fori(0, QUARTERS - 1) as i:
                if reads_stacks:
                    eng.wait_ge(stack_in, i * (32 * SLOTS) + 64 * SLOTS)
                for k in range(1, 5):
                    body(i * 4 + k, k % 2)
            for j in range(TILES - 3, TILES):
                body(j, j % 2)

        def s1_chunks(b, g):
            return [(*neighbour(b, g, 1), n) for n in range(S1_AHEAD, UC)] + \
                   [(*neighbour(b, g, 2), n) for n in range(S1_AHEAD)]

        @block.sync
        def _(sp):
            sp.dma_start(x_all[:], t["x"].rearrange("(n p) c -> p n c", p=128)).then_inc(load, 16)
            sp.dma_start(ident[:], t["ident"]).then_inc(load, 16)
            sp.dma_start(head_rows[:], t["head_rows"]).then_inc(load, 16)
            sp.dma_start(BQ, t["bq"]).then_inc(load, 16)
            sp.dma_start(WqT[:], t["WqT"]).then_inc(w_in, 16)
            sp.dma_start(WkT[:], t["WkT"]).then_inc(w_in, 16)
            sp.dma_start(BK, t["bk"]).then_inc(w_in, 16)
            sp.dma_start(ctxT[:, 0, :], t["ctxT"][0]).then_inc(ctx_in[0], 16)
            sp.dma_start(ctxT[:, 1, :], t["ctxT"][1]).then_inc(ctx_in[1], 16)
            sp.dma_start(WvT[:], t["WvT"]).then_inc(w_in, 16)
            sp.dma_start(WoP[:], t["WoP"]).then_inc(w_in, 16)
            sp.dma_start(bvc[:], t["bv"]).then_inc(w_in, 16)
            sp.dma_start(WoT[:], t["WoT"]).then_inc(w_in, 16)

            def stack_all(s0, d0, parts, part_of, dst, done):
                for part in range(3):
                    sp.wait_ge(split, s0 + [1, 3, 4][part])
                    sp.dma_start(qd[part], parts[:, part, :]).then_inc(qd_in, 16)
                    sp.wait_ge(qd_in, 16 * (d0 + part + 1))
                    for s in range(SLOTS):
                        if part_of[s] == part:
                            sp.dma_start(dst[16 * s:16 * s + 16, :, :],
                                         qd[part].rearrange("(p r) t -> r p t", r=16)).then_inc(done, 16)

            stack_all(0, 0, qparts0, Q_PART, Qall, qst_in)

            def parts_out(b):
                for c, (at, w) in enumerate(CUTS):
                    wait_alone(sp, klo_done, count(lambda n: NCUT * n + c + 1, b))
                    sp.dma_start(kd[parity(b)].rearrange("k r m -> r k m")[:, :, at:at + w],
                                 Kpart[:, parity(b), :, at:at + w]).then_inc(kd_in[parity(b)], 16)
                wait_alone(sp, kd_in[parity(b)], count(lambda n: 16 * NCUT * (n // 2 + 1), b))

            def k_stack(b, g):
                if there(b, 2, B):
                    wait_alone(sp, s2_done, count(lambda n: MT * (2 * (n - 2) + g + 1), b))
                for s in range(SLOTS):
                    sp.dma_start(Kst[16 * s:16 * s + 16, parity(b), GP * g:GP * g + GP, 0:M],
                                 kd[parity(b), K_PART[s], 64 * g:64 * g + 64].rearrange("(p r) m -> r p m", r=16))\
                      .then_inc(kst_in[parity(b)][g], 16)

            def context(b):
                wait_alone(sp, bank_full, count(lambda n: 1 + USE["v", n, NV - 1], b - 2))
                sp.dma_start(ctxT[:, parity(b), :],
                             t["ctxT"][bass.ds(value(b), 1)].rearrange("o c m -> (o c) m"))\
                  .then_inc(ctx_in[parity(b)], 16)

            parts_out(0)
            for g in range(GROUPS):
                k_stack(0, g)
            context(2)
            parts_out(1)
            for g in range(GROUPS):
                k_stack(1, g)

            def batch(b):
                if there(b, 0, B - 2):
                    parts_out(b + 2)
                if there(b, 0, B - 3):
                    context(b + 3)
                if there(b, 0, B - 2):
                    for g in range(GROUPS):
                        k_stack(b + 2, g)

            over_batches(sp, batch)

            sp.wait_ge(x1_done, B)
            for n, name in enumerate(("wqT", "wk", "wvT")):
                sp.dma_start(lw[:, n, :], t[name]).then_inc(sw_in, 16)
            sp.dma_start(lw[:, 7, :], t["head_block"]).then_inc(sw_in, 16)
            for n, name in enumerate(("aqT", "bbq", "avT", "bbv")):
                sp.dma_start(lora[:, n, :], t[name]).then_inc(sw_in, 16)
            sp.dma_start(SBQ, t["sbq"]).then_inc(sw_in, 16)
            sp.dma_start(SBK, t["sbk"]).then_inc(sw_in, 16)
            sp.dma_start(sbvc[:], t["sbv"]).then_inc(sw_in, 16)
            sp.dma_start(Wp[:], t["Wp"]).then_inc(sw_in, 16)
            sp.dma_start(bp[:], t["bp"].to_broadcast((128, C))).then_inc(sw_in, 16)
            sp.dma_start(batch_ones[:], t["batch_ones"]).then_inc(sw_in, 16)
            sp.dma_start(WpE[:], t["WpE"]).then_inc(sw_in, 16)
            def quarter_out(q):
                for w in range(2):
                    sp.wait_ge(parts_done, 3 * (2 * q + w) + 3)
                    sp.dma_start(sd[w].rearrange("k r m -> r k m")[:, :, QW * q:QW * q + QW], qkparts[:, q % 2, w])\
                      .then_inc(sd_in[q % 2], 16)

            quarter_out(0)
            for q in range(QUARTERS):
                if q + 1 < QUARTERS:
                    quarter_out(q + 1)
                sp.wait_ge(sd_in[q % 2], 32 * (q // 2 + 1))
                if q:
                    sp.wait_ge(stack_in, 32 * SLOTS * q)
                for dst, w, part_of in ((Qall, 0, Q_PART), (Kall, 1, K_PART)):
                    for n in range(SLOTS):
                        sp.dma_start(dst[16 * n:16 * n + 16, :, QW * q:QW * q + QW],
                                     sd[w, part_of[n], :, QW * q:QW * q + QW].rearrange("(p r) t -> r p t", r=16))\
                          .then_inc(stack_in, 16)
            for name, dst in (("gateT", gateT), ("iota", iota), ("W1T", W1T), ("W3T", W3T), ("W2T", W2T)):
                sp.dma_start(dst[:], t[name]).then_inc(fw_in, 16)
            with sp.Fori(0, CHUNKS // 2) as i:
                for k in range(2):
                    wait_alone(sp, o_done, i * 2 + k + 1)
                    sp.dma_start(out[bass.ds(i * (2 * CHUNK) + k * CHUNK, CHUNK), :].rearrange("(n p) c -> p n c", p=128),
                                 out_t[:, k]).then_inc(o_out[k], 16)
            for k in range(2):
                sp.wait_ge(o_out[k], 16 * (CHUNKS // 2))

        @block.gpsimd
        def _(pool):
            for n in range(2):
                nc.gpsimd.memset(Kst[96:99, n, :, :], 1.0).then_inc(pads, 1)
                pool.wait_ge(pads, 2 * n + 1)
                nc.gpsimd.memset(Kst[0:96, n, :, M:MPAD], 0.0).then_inc(pads, 1)
                pool.wait_ge(pads, 2 * n + 2)
            pool.wait_ge(ln_tr, TILES // 4)
            for n in range(2):
                nc.gpsimd.memset(V[:, n, :, :, 16:32], 1.0).then_inc(pads, 1)
                pool.wait_ge(pads, n + 5)

            def k_parts(b, c):
                at, w = CUTS[c]
                done = count(lambda n: NCUT * n + c + 1, b)
                pool.wait_ge(kf_done, done)
                nc.gpsimd.tensor_tensor(Krest[:, c % 2, 0:w], Krest[:, c % 2, 0:w], Kpart[:, parity(b), 0, at:at + w],
                                        ALU.subtract).then_inc(krest_done, 1)
                pool.wait_ge(kmid_done, done)
                nc.gpsimd.tensor_tensor(Kpart[:, parity(b), 2, at:at + w], Krest[:, c % 2, 0:w],
                                        Kpart[:, parity(b), 1, at:at + w], ALU.subtract).then_inc(klo_done, 1)
                pool.wait_ge(klo_done, done)

            def divide(b, g):
                pool.wait_ge(den_done, units(b, g)(2, 2))
                nc.gpsimd.tensor_tensor(On[:, g, :], O[:, g, :], den[:, g, :], ALU.mult).then_inc(norm_done, 1)
                pool.wait_ge(norm_done, units(b, g)(1, 1))

            for b in range(2):
                for c in range(NCUT):
                    k_parts(b, c)

            def batch(b):
                if there(b, 1, B):
                    divide(b - 1, 0)
                if there(b, 0, B - 2):
                    for c in range(NCUT):
                        k_parts(b + 2, c)
                if there(b, 1, B):
                    divide(b - 1, 1)

            over_batches(pool, batch)
            for g in range(GROUPS):
                divide(B - 1, g)
            pool.wait_ge(x1_done, B)
            nc.gpsimd.memset(Vall[:].rearrange("p a b c -> p (a b c)"), 0.0).then_inc(pads, 1)
            pool.wait_ge(pads, 7)
            nc.gpsimd.memset(K2st[96:99, :, :, :].rearrange("p a b c -> p (a b c)"), 1.0).then_inc(pads, 1)
            pool.wait_ge(pads, 8)
            pool.wait_ge(lora_ev, 9)
            pool.wait_ge(ln_stat, 2 * LN_STEPS)
            nc.gpsimd.tensor_tensor(x_all[:], x_all[:], bo2[:].unsqueeze(1).broadcast_to((128, TILES, C)), ALU.add)\
              .then_inc(x_b, 1)

            def key_stack(j, par):
                wait(pool, b_kst, j)
                if not isinstance(j, int) or j >= 2:
                    pool.wait_ge(b_s2, j - 1)
                nc.gpsimd.tensor_copy(K2st[0:ROWS, par, :, :], Kall[0:ROWS, :, bass.ds(j * 128, 128)])\
                  .then_inc(b_kst, 1)

            def pair(j, par):
                if exists(j + 3):
                    key_stack(j + 3, 1 - par)

            pool.wait_ge(x_b, 1)
            pool.wait_ge(stack_in, 32 * SLOTS)
            for j in range(3):
                key_stack(j, j % 2)
            over_pairs(pool, pair)

        @block.tensor
        def _(pe):
            mm = nc.tensor.matmul

            def turn_tiles(k, xn):
                for q in range(TILES // 4):
                    pe.wait_ge(ln_stat, LN_STEPS * k + 3 + q + 1)
                    for j in range(4):
                        last = nc.tensor.transpose(ps[:, q % 4, 128 * j:128 * j + 128], xn[:, 4 * q + j, :], ident[:])
                    last.then_inc(ln_tr, 1)

            turn_tiles(0, xn0)
            pe.wait_ge(w_in, 16 * N_W)
            for q in range(4):
                pe.wait_ge(ln_ev, q + 1)
                mm(ps[:, 4 + q, :], WqT[:], xnT0[:, 512 * q:512 * q + 512], start=True, stop=True).then_inc(proj, 1)

            def bank(kind, b, c):
                some = b if isinstance(b, int) else b.off + 2 * FIRST
                if USE[kind, some, c] == 0:
                    return
                last, bb, cc = ORDER[USE[kind, some, c] - 1]
                read, of_batch = {"k": (kf_done, NCUT), "v": (v_done, NV), "m": (max_rows, GROUPS), "y": (x1_done, 1)}[last]
                pe.wait_ge(read, count(lambda n: of_batch * (n + bb - some) + cc + 1, b))

            def k_chunk(b, c):
                at, w = CUTS[c]
                bank("k", b, c)
                if c == 0:
                    pe.wait_ge(ctx_in[parity(b)], count(lambda n: 16 * (n // 2 + 1), b))
                mm(psM[:, 0:w], WkT[:], ctxT[:, parity(b), at:at + w], start=True, stop=True).then_inc(bank_full, 1)

            def v_chunk(b, c):
                bank("v", b, c)
                if c == 0:
                    pe.wait_ge(ctx_in[parity(b)], count(lambda n: 16 * (n // 2 + 1), b))
                for m in range(VT * c, min(VT * c + VT, MT)):
                    w = 128 if m < MT - 1 else LAST_ROWS
                    last = mm(psM[0:w, 128 * (m - VT * c):128 * (m - VT * c) + 128],
                              ctxT[:, parity(b), 128 * m:128 * m + w], WvT[:], start=True, stop=True)
                last.then_inc(bank_full, 1)

            def s1(b, g, n):
                u = units(b, g)
                j, c = divmod(n, NCUT)
                at, w = CUTS[c]
                if n == 0:
                    pe.wait_ge(qst_done, u(1, 1))
                    pe.wait_ge(kst_in[parity(b)][g], count(lambda k: 16 * SLOTS * (k // 2 + 1), b))
                wait(pe, max_done, u(UC, n + 1 - S1_BACK[n]))
                mm(psS1[:, S1_BANK[n], 0:w], Qst[0:ROWS, parity(b), g, j, :], Kst[0:ROWS, parity(b), GP * g + j, at:at + w],
                   start=True, stop=True).then_inc(s1_done, 1)

            def max_to_rows(b, g):
                bank("m", b, g)
                pe.wait_ge(nm_chain, units(b, g)(5, 5))
                for j in range(GP):
                    last = mm(psM[96:99, 128 * j:128 * j + 128], nmp[:, g, j, :], identb[:], start=True, stop=True)
                last.then_inc(bank_full, 1)

            def s2(b, g, m):
                u = units(b, g)
                if m == 0:
                    pe.wait_ge(max_rows, u(1, 1))
                wait(pe, exp_done, u(MT, m + 1 - S2_BACK[g][m]))
                for j in range(GP):
                    last = mm(psS2[:, (m + g) % 3, 128 * j:128 * j + 128],
                              Kst[0:ROWS + 3, parity(b), GP * g + j, 128 * m:128 * m + 128],
                              Qst[0:ROWS + 3, parity(b), g, j, :], start=True, stop=True)
                last.then_inc(s2_done, 1)

            def av(b, g, m):
                u = units(b, g)
                if m == 0:
                    pe.wait_ge(v_done, count(lambda n: NV * (n + 1), b))
                    wait(pe, o_read, u(1, 0))
                pe.wait_ge(exp_done, u(MT, m + 1))
                w = 128 if m < MT - 1 else LAST_ROWS
                for j in range(GP):
                    last = mm(psO[32 * j:32 * j + 32, 0:128], V[0:w, parity(b), m, GP * g + j, :],
                              P[0:w, m, 128 * j:128 * j + 128], start=(m == 0), stop=(m == MT - 1))
                last.then_inc(av_done, 1)

            def project_out(b):
                bank("y", b, 0)
                pe.wait_ge(norm_done, units(b, 1)(1, 1))
                r = N * parity(b)
                for g in range(GROUPS):
                    for h in range(2):
                        last = mm(psM[r:r + N, 0:C], On[:, g, N * h:N * h + N], WoP[:, g, h, :],
                                  start=(g == 0 and h == 0), stop=(g == 1 and h == 1))
                last.then_inc(bank_full, 1)

            pe.wait_ge(proj_ev, 4)
            mm(ps[:, 4, 0:128], bvc[:], WoT[:], start=True, stop=True).then_inc(bo_pe, 1)
            for b in range(2):
                for c in range(NCUT):
                    k_chunk(b, c)
            for c in range(NV):
                v_chunk(0, c)
            pe.wait_ge(pads, 6)
            pe.wait_ge(made, 1)
            for n in range(UC):
                s1(0, 0, n)
            max_to_rows(0, 0)
            for n in range(S1_AHEAD):
                s1(0, 1, n)

            def step(b, g):
                prev, nxt = neighbour(b, g, -1), neighbour(b, g, 1)
                todo = s1_chunks(b, g)
                for m in range(MT):
                    s2(b, g, m)
                    if m and there(prev[0], 0, B):
                        av(*prev, m)
                    for _ in range(S1_AT[m]):
                        bb, gg, n = todo.pop(0)
                        if there(bb, 0, B):
                            s1(bb, gg, n)
                    if m == 0 and there(prev[0], 0, B):
                        av(*prev, 0)
                    if m == M_AT and there(nxt[0], 0, B):
                        max_to_rows(*nxt)
                    if g == 1 and m == Y_AT and there(b, 1, B):
                        project_out(b - 1)
                    if g == 0 and m in K_AT and there(b, 0, B - 2):
                        k_chunk(b + 2, K_AT[m])
                    if g == 1 and m in V_AT and there(b, 0, B - 1):
                        v_chunk(b + 1, V_AT[m])

            def batch(b):
                for g in range(GROUPS):
                    step(b, g)

            over_batches(pe, batch)
            for m in range(MT):
                av(B - 1, 1, m)
            project_out(B - 1)

            turn_tiles(1, xn1)
            pe.wait_ge(sw_in, 16 * N_SW)
            mm(ps[:, 4, 0:128], lora[:, 0, :], lora[:, 1, :], start=True, stop=True)
            mm(ps[:, 5, 0:128], lora[:, 2, :], lora[:, 3, :], start=True, stop=True).then_inc(lora_pe, 1)
            pe.wait_ge(lora_ev, 4)
            mm(ps[:, 6, 0:128], lw[:, 0, :], lw[:, 5, :], start=True, stop=True)
            mm(ps[:, 6, 128:256], lw[:, 2, :], lw[:, 6, :], start=True, stop=True)
            mm(ps[:, 6, 256:384], lw[:, 6, :], sbvc[:], start=True, stop=True)
            mm(ps[:, 6, 384:386], lw[:, 5, :], biases[:, 2:4], start=True, stop=True).then_inc(lora_pe, 1)
            pe.wait_ge(lora_ev, 8)
            mm(ps[:, 7, 0:128], bv2[:], Wp[:], start=True, stop=True).then_inc(lora_pe, 1)
            for q in range(QUARTERS):
                pe.wait_ge(ln_ev, 4 + max(q, 1) + 1)
                for w in range(2):
                    if q >= 2:
                        pe.wait_ge(f_done, 2 * (q - 2) + w + 1)
                    mm(ps[:, [4, 0][q % 2] + w, :], lw[:, 3 if w == 0 else 1, :], xnT1[:, QW * q:QW * q + QW],
                       start=True, stop=True).then_inc(p_full, 1)
                if q == 1:
                    pe.wait_ge(lora_ev, 9)
                if q >= 2:
                    pe.wait_ge(vals, q - 1)
                for j in range(4):
                    m = 4 * q + j
                    last = mm(ps[:, 6 + q % 2, 128 * j:128 * j + 128], xnT1[:, 128 * m:128 * m + 128], lw[:, 4, :],
                              start=True, stop=True)
                last.then_inc(p_full, 1)

            def scores_for_max(j, par):
                pe.wait_ge(b_st, j + 1)
                pe.wait_ge(b_kst, j + 1)
                if not isinstance(j, int) or j:
                    pe.wait_ge(b_rows, j * 2 - 1)
                for e in range(2):
                    for p in range(PAIRS):
                        last = mm(ps[:, e, N * p:N * p + N], Q2st[0:ROWS, par, e, p, :],
                                  K2st[0:ROWS, par, p, N * e:N * e + N], start=True, stop=True)
                last.then_inc(b_s1, 1)

            def rows_of_max(j, par):
                pe.wait_ge(b_chain, j * 5 + 5)
                wait(pe, b_rows, j * 2)
                for e in (1, 0):
                    for p in range(PAIRS):
                        last = mm(ps[96:99, 2 * (1 - e) + p // 4, 128 * (p % 4):128 * (p % 4) + 128],
                                  nmp2[:, par, PAIRS * e + p, :], identb[:], start=True, stop=True)
                    last.then_inc(b_nm, 1)

            def shifted_scores(j, par):
                pe.wait_ge(b_rows, j * 2 + 2)
                wait(pe, b_exp, j)
                for e in range(2):
                    for p in range(PAIRS):
                        last = mm(ps[N * e:N * e + N, 4 + p // 4, 128 * (p % 4):128 * (p % 4) + 128],
                                  K2st[0:ROWS + 3, par, p, N * e:N * e + N], Q2st[0:ROWS + 3, par, e, p, :],
                                  start=True, stop=True)
                last.then_inc(b_s2, 1)

            def values(j, par):
                pe.wait_ge(b_exp, j + 1)
                pe.wait_ge(b_v, j + 1)
                wait(pe, b_norm, j * 2)
                for at, ones in ((0, False), (256, True)):
                    for p in range(PAIRS):
                        q = 32 * (p % 4)
                        last = mm(ps[q:q + 32, 6, at + 128 * (p // 4):at + 128 * (p // 4) + 128],
                                  batch_ones[:] if ones else V2st[:, par, p, :], P2[:, par, p, :],
                                  start=True, stop=True)
                last.then_inc(b_av, 1)

            def outputs(j, par):
                pe.wait_ge(b_norm, j * 2 + 2)
                wait(pe, b_x, j)
                for e in range(2):
                    for g in range(GROUPS):
                        for h in range(2):
                            last = mm(ps[N * e:N * e + N, 7, 0:C], On2[:, par, g, N * h:N * h + N], WpE[:, g, e, h, :],
                                      start=(g == 0 and h == 0), stop=(g == 1 and h == 1))
                last.then_inc(b_y, 1)

            pe.wait_ge(f_done, 2 * QUARTERS)
            pe.wait_ge(vals, QUARTERS)
            pe.wait_ge(pads, 8)
            scores_for_max(0, 0)
            rows_of_max(0, 0)
            scores_for_max(1, 1)
            shifted_scores(0, 0)
            rows_of_max(1, 1)

            def pair(j, par):
                if exists(j + 2):
                    scores_for_max(j + 2, par)
                if exists(j + 1):
                    shifted_scores(j + 1, 1 - par)
                values(j, par)
                if exists(j + 2):
                    rows_of_max(j + 2, par)
                if exists(j - 1):
                    outputs(j - 1, 1 - par)

            over_pairs(pe, pair)
            outputs(TILES - 1, 1)

            turn_tiles(2, xn1)
            pe.wait_ge(ln_ev, 12)
            pe.wait_ge(fw_in, 16 * 5)
            for m in range(TILES):
                last = mm(ps[:, 4, 8 * m:8 * m + 8], xnT1[:, 128 * m:128 * m + 128], gateT[:], start=True, stop=True)
            last.then_inc(g_pe, 1)

            def hidden(q, e, m):
                n = q * (EXPERTS * HT) + (HT * e + m)
                if not isinstance(n, int) or n >= 2:
                    pe.wait_ge(h_done, n - 1)
                x_q = xnT1[:, bass.ds(q * CHUNK, CHUNK)]
                mm(ps[:, m % 2, :], W1T[:, e, 128 * m:128 * m + 128], x_q, start=True, stop=True)
                mm(ps[:, 2 + m % 2, :], W3T[:, e, 128 * m:128 * m + 128], x_q, start=True, stop=True).then_inc(h_pe, 1)

            def expert_out(q, e):
                n = q * EXPERTS + e
                pe.wait_ge(h_done, n * HT + HT)
                if not isinstance(n, int) or n >= 2:
                    pe.wait_ge(y_done, n - 1)
                for k in range(CT):
                    for m in range(HT):
                        last = mm(ps[:, 5 + e % 2, 128 * k:128 * k + 128], hT[:, e % 2, m, 128 * k:128 * k + 128],
                                  W2T[:, e, m, :], start=(m == 0), stop=(m == HT - 1))
                last.then_inc(y_pe, 1)

            def chunk(q, before):
                for e in range(EXPERTS):
                    for m in range(HT):
                        hidden(q, e, m)
                        if m == 1:
                            if e:
                                expert_out(q, e - 1)
                            elif before is not None:
                                expert_out(before, EXPERTS - 1)

            chunk(0, None)
            with pe.Fori(1, CHUNKS) as q:
                chunk(q, q - 1)
            expert_out(CHUNKS - 1, EXPERTS - 1)

        @block.scalar
        def _(act):
            def deviations(k):
                act.wait_ge(ln_stat, LN_STEPS * k + 2)
                nc.scalar.activation(std[:], mv[:, :, 1], ACT.Sqrt, bias=eps[:, 0:1]).then_inc(ln_std, 1)

            def evacuate(k, xnT):
                for q in range(TILES // 4):
                    act.wait_ge(ln_tr, k * (TILES // 4) + q + 1)
                    nc.scalar.activation(xnT[:, 512 * q:512 * q + 512], ps[:, q, :], ACT.Copy).then_inc(ln_ev, 1)

            deviations(0)
            evacuate(0, xnT0)

            def k_in(b, c):
                at, w = CUTS[c]
                if c == 0 and there(b, 2, B):
                    act.wait_ge(kd_in[parity(b)], count(lambda n: 16 * NCUT * (n // 2), b))
                act.wait_ge(bank_full, count(lambda n: USE["k", n, c] + 1, b))
                nc.scalar.activation(Kpart[:, parity(b), 0, at:at + w], psM[:, 0:w], ACT.Identity,
                                     bias=BK).then_inc(khi_done, 1)
                wait(act, klo_done, count(lambda n: NCUT * n + c - 1, b))
                nc.scalar.activation(Krest[:, c % 2, 0:w], psM[:, 0:w], ACT.Identity, bias=BK).then_inc(kf_done, 1)

            def v_in(b, c):
                n = min(VT, MT - VT * c)
                w = 128 if c < NV - 1 else LAST_ROWS
                act.wait_ge(bank_full, count(lambda k: USE["v", k, c] + 1, b))
                nc.scalar.activation(V[0:w, parity(b), VT * c:VT * c + n, :, 0:16],
                                     psM[0:w, 0:128 * n].rearrange("p (m a k) -> p m a k", a=PAIRS, k=16),
                                     ACT.Copy).then_inc(v_done, 1)

            def exp(b, g, m):
                u = units(b, g)
                act.wait_ge(s2_done, u(MT, m + 1))
                wait(act, av_done, u(MT, m + 1 - MT))
                nc.scalar.activation(P[:, m, :], psS2[:, (m + g) % 3, :], ACT.Exp).then_inc(exp_done, 1)

            def rows(b, g):
                act.wait_ge(bank_full, count(lambda n: USE["m", n, g] + 1, b))
                act.wait_ge(qst_done, units(b, g)(1, 1))
                nc.scalar.activation(Qst[96:99, parity(b), g, :, :], psM[96:99, :].rearrange("p (j q) -> p j q", j=GP),
                                     ACT.Copy).then_inc(max_rows, 1)

            def read_out(b, g):
                u = units(b, g)
                act.wait_ge(av_done, u(MT, MT))
                wait(act, norm_done, u(1, -1))
                nc.scalar.activation(O[:, g, :], psO[:, 0:128], ACT.Copy).then_inc(o_read, 1)

            act.wait_ge(w_in, 16 * N_W)
            for b in range(2):
                for c in range(NCUT):
                    k_in(b, c)
            act.wait_ge(pads, 6)
            for c in range(NV):
                v_in(0, c)
            rows(0, 0)
            act.wait_ge(qst_in, 16 * SLOTS)

            def batch(b):
                for g in range(GROUPS):
                    for m in range(MT):
                        prev = neighbour(b, g, -1)
                        if m == MT - 1 and there(prev[0], 0, B):
                            read_out(*prev)
                        nxt = neighbour(b, g, 1)
                        if m == M_AT + 1 and there(nxt[0], 0, B):
                            rows(*nxt)
                        exp(b, g, m)
                        if g == 0 and m in K_AT and there(b, 0, B - 2):
                            k_in(b + 2, K_AT[m])
                        if g == 1 and m in V_AT and there(b, 0, B - 1):
                            v_in(b + 1, V_AT[m])

            over_batches(act, batch)
            read_out(B - 1, 1)

            deviations(1)
            evacuate(1, xnT1)

            for q in range(QUARTERS):
                for w in range(2):
                    act.wait_ge(p_full, 3 * q + w + 1)
                    if q >= 2:
                        act.wait_ge(sd_in[q % 2], 32 * (q // 2))
                    some = ps[:, [4, 0][q % 2] + w, :]
                    bias, scale = ((SBQ2, SCALE), (SBK, 1.0))[w]
                    nc.scalar.activation(qkparts[:, q % 2, w, 0, :], some, ACT.Identity, bias=bias, scale=scale)\
                      .then_inc(hi_done, 1)
                    nc.scalar.activation(qk[:, q % 2, w, :], some, ACT.Identity, bias=bias, scale=scale)\
                      .then_inc(f_done, 1)
                if q == 0:
                    act.wait_ge(pads, 7)
                act.wait_ge(p_full, 3 * q + 3)
                for e in range(2):
                    last = nc.scalar.activation(
                        Vall[N * e:N * e + N, 4 * q:4 * q + 4, :, 2 * D * e:2 * D * e + 2 * D],
                        ps[N * e:N * e + N, 6 + q % 2, :].rearrange("p (j a k) -> p j a k", j=4, a=PAIRS), ACT.Copy)
                last.then_inc(vals, 1)

            def rows_in(j, par):
                for n, e in enumerate((1, 0)):
                    act.wait_ge(b_nm, j * 2 + n + 1)
                    nc.scalar.activation(Q2st[96:99, par, e, :, :],
                                         ps[96:99, 2 * n:2 * n + 2, :].rearrange("p a (b q) -> p (a b) q", b=4),
                                         ACT.Copy).then_inc(b_rows, 1)

            def exponentials(j, par):
                act.wait_ge(b_s2, j + 1)
                if not isinstance(j, int) or j > 1:
                    act.wait_ge(b_av, j - 1)
                nc.scalar.activation(P2[:, par].rearrange("p a b -> p (a b)"),
                                     ps[:, 4:6, :].rearrange("p a b -> p (a b)"), ACT.Exp).then_inc(b_exp, 1)

            def values_in(j, par):
                nc.scalar.activation(V2st[:, par].rearrange("p a b -> p (a b)"),
                                     Vall[:, bass.ds(j, 1)].rearrange("p o a b -> p (o a b)"), ACT.Copy)\
                  .then_inc(b_v, 1)

            rows_in(0, 0)
            act.wait_ge(vals, QUARTERS)
            exponentials(0, 0)
            values_in(0, 0)
            rows_in(1, 1)

            def pair(j, par):
                if exists(j + 1):
                    exponentials(j + 1, 1 - par)
                    values_in(j + 1, 1 - par)
                if exists(j + 2):
                    rows_in(j + 2, par)

            over_pairs(act, pair)

            deviations(2)
            evacuate(2, xnT1)

            def silu(q, e, m):
                n = q * (EXPERTS * HT) + (HT * e + m)
                act.wait_ge(h_pe, n + 1)
                if not isinstance(n, int) or n >= 2:
                    act.wait_ge(h_done, n - 1)
                nc.scalar.activation(sil[:, m % 2, :], ps[:, m % 2, :], ACT.Silu).then_inc(h_sil, 1)

            def chunk(q):
                for e in range(EXPERTS):
                    for m in range(HT):
                        silu(q, e, m)
                        if isinstance(q, int) and e == 0 and m == 1:
                            act.wait_ge(g_chain, 4)
                            nc.scalar.activation(tw[:, 1, :], tw[:, 0, :], ACT.Exp).then_inc(g_exp, 1)

            chunk(0)
            with act.Fori(1, CHUNKS) as q:
                chunk(q)

        @block.vector
        def _(dve):
            v = nc.vector
            v.memset(eps[:], EPS)
            dve.wait_ge(load, 16 * N_LOAD)
            v.tensor_copy(identb[:], ident[:]).then_inc(made, 1)

            def normalise(k, xn):
                s0 = LN_STEPS * k
                for m in range(TILES):
                    last = v.bn_stats(stats[:, m, :], x_all[:, m, :])
                last.then_inc(ln_stat, 1)
                dve.wait_ge(ln_stat, s0 + 1)
                for m in range(TILES):
                    last = v.bn_aggr(mv[:, m, :], stats[:, m, :])
                last.then_inc(ln_stat, 1)
                dve.wait_ge(ln_std, k + 1)
                v.reciprocal(rstd[:], std[:]).then_inc(ln_stat, 1)
                dve.wait_ge(ln_stat, s0 + 3)
                for m in range(TILES):
                    last = v.tensor_scalar(xn[:, m, :], x_all[:, m, :], mv[:, m, 0:1], rstd[:, m:m + 1],
                                           ALU.subtract, ALU.mult)
                    if m % 4 == 3:
                        last.then_inc(ln_stat, 1)

            def project_and_split(n0, s0, bias, scale, qf, parts):
                for q in range(4):
                    dve.wait_ge(proj, n0 + q + 1)
                    v.tensor_scalar(qf[:, 512 * q:512 * q + 512], ps[:, 4 + q, :], bias, scale,
                                    ALU.add, ALU.mult).then_inc(proj_ev, 1)
                dve.wait_ge(proj_ev, n0 + 4)
                v.tensor_copy(parts[:, 0, :], qf).then_inc(split, 1)
                dve.wait_ge(split, s0 + 1)
                v.tensor_tensor(qf, qf, parts[:, 0, :], ALU.subtract).then_inc(split, 1)
                dve.wait_ge(split, s0 + 2)
                v.tensor_copy(parts[:, 1, :], qf).then_inc(split, 1)
                dve.wait_ge(split, s0 + 3)
                v.tensor_tensor(parts[:, 2, :], qf, parts[:, 1, :], ALU.subtract).then_inc(split, 1)

            normalise(0, xn0)
            project_and_split(0, 0, BQ, SCALE, qf0, qparts0)

            def k_mid(b, c):
                at, w = CUTS[c]
                dve.wait_ge(krest_done, count(lambda n: NCUT * n + c + 1, b))
                v.tensor_copy(Kpart[:, parity(b), 1, at:at + w], Krest[:, c % 2, 0:w]).then_inc(kmid_done, 1)

            def query_stack(b, g):
                u = units(b, g)
                wait(dve, s2_done, u(MT, -3 * MT))
                for h in range(2):
                    last = v.tensor_scalar(Qst[0:ROWS, parity(b), g, :, N * h:N * h + N],
                                           Qall[0:ROWS, GP * g:GP * g + GP, bass.ds(value(b) * N, N)],
                                           head_rows[0:ROWS, h:h + 1], None, ALU.mult)
                last.then_inc(qst_done, 1)

            def chunk_max(b, g, n):
                j, c = divmod(n, NCUT)
                dve.wait_ge(s1_done, units(b, g)(UC, n + 1))
                v.tensor_reduce(mxc[:, g, j, c:c + 1], psS1[:, S1_BANK[n], 0:CUTS[c][1]], AX.X, ALU.max)\
                 .then_inc(max_done, 1)

            def split_max(b, g):
                u = units(b, g)
                dve.wait_ge(max_done, u(UC, UC))
                v.tensor_reduce(nmf[:, g, :], mxc[:, g, :, :], AX.X, ALU.max, negate=True).then_inc(nm_chain, 1)
                dve.wait_ge(nm_chain, u(5, 1))
                v.tensor_copy(nmp[:, g, :, 0], nmf[:, g, :]).then_inc(nm_chain, 1)
                dve.wait_ge(nm_chain, u(5, 2))
                v.tensor_tensor(nmf[:, g, :], nmf[:, g, :], nmp[:, g, :, 0], ALU.subtract).then_inc(nm_chain, 1)
                dve.wait_ge(nm_chain, u(5, 3))
                v.tensor_copy(nmp[:, g, :, 1], nmf[:, g, :]).then_inc(nm_chain, 1)
                dve.wait_ge(nm_chain, u(5, 4))
                v.tensor_tensor(nmp[:, g, :, 2], nmf[:, g, :], nmp[:, g, :, 1], ALU.subtract).then_inc(nm_chain, 1)

            def sums_up(b, g):
                u = units(b, g)
                wait_alone(dve, o_read, u(1, 1))
                v.stream_shuffle(den[:, g, :], O[:, g, :], SUM_ROWS).then_inc(den_done, 1)
                dve.wait_ge(den_done, u(2, 1))
                v.reciprocal(den[:, g, :], den[:, g, :]).then_inc(den_done, 1)

            def residual(b):
                dve.wait_ge(bank_full, count(lambda n: USE["y", n, 0] + 1, b))
                r = N * parity(b)
                m = bass.ds(value(b - parity(b)) // 2, 1) if isinstance(b, int) else bass.ds(b.i + b.off // 2, 1)
                x = x_all[r:r + N, m, :].rearrange("p o c -> p (o c)")
                v.tensor_tensor(x, psM[r:r + N, 0:C], x, ALU.add).then_inc(x1_done, 1)

            dve.wait_ge(bo_pe, 1)
            v.tensor_copy(bo[:], ps[:, 4, 0:128]).then_inc(bo_done, 1)
            dve.wait_ge(bo_done, 1)
            v.tensor_tensor(x_all[:], x_all[:], bo[:].unsqueeze(1).broadcast_to((128, TILES, C)), ALU.add)\
             .then_inc(bo_done, 1)
            dve.wait_ge(bo_done, 2)
            for b in range(2):
                for c in range(NCUT):
                    k_mid(b, c)
            dve.wait_ge(qst_in, 16 * SLOTS)
            for g in range(GROUPS):
                query_stack(0, g)
            for n in range(UC):
                chunk_max(0, 0, n)
            split_max(0, 0)
            for n in range(S1_AHEAD):
                chunk_max(0, 1, n)

            def step(b, g):
                nxt, old = neighbour(b, g, 1), neighbour(b, g, -2)
                todo = s1_chunks(b, g)
                for m in range(MT):
                    for _ in range(S1_AT[m]):
                        bb, gg, n = todo.pop(0)
                        if there(bb, 0, B):
                            chunk_max(bb, gg, n)
                        if n == UC - 1 and there(bb, 0, B):
                            split_max(bb, gg)
                    if m == 1 and there(old[0], 0, B):
                        sums_up(*old)
                    if m == QST_AT and there(b, 0, B - 1):
                        query_stack(b + 1, g)
                    if (g, m) in KMID_AT and there(b, 0, B - 2):
                        k_mid(b + 2, KMID_AT[g, m])
                    if g == 1 and m == Y_AT + 1 and there(b, 1, B):
                        residual(b - 1)

            def batch(b):
                for g in range(GROUPS):
                    step(b, g)

            over_batches(dve, batch)
            for g in range(GROUPS):
                sums_up(B - 1, g)
            residual(B - 1)

            dve.wait_ge(x1_done, B)
            normalise(1, xn1)
            dve.wait_ge(sw_in, 16 * N_SW)
            dve.wait_ge(lora_pe, 1)
            for n in range(2):
                v.tensor_tensor(lw[:, 8 + n, :], ps[:, 4 + n, 0:128], lw[:, 7, :], ALU.mult).then_inc(lora_ev, 1)
            dve.wait_ge(lora_ev, 2)
            for n in range(2):
                v.scalar_tensor_tensor(lw[:, 5 + n, :], lw[:, 8 + n, :], LORA, ident[:],
                                       ALU.mult, ALU.add).then_inc(lora_ev, 1)
            dve.wait_ge(lora_pe, 2)
            v.tensor_copy(lw[:, 3, :], ps[:, 6, 0:128]).then_inc(lora_ev, 1)
            v.tensor_copy(lw[:, 4, :], ps[:, 6, 128:256]).then_inc(lora_ev, 1)
            v.tensor_copy(bv2[:], ps[:, 6, 256:384]).then_inc(lora_ev, 1)
            v.tensor_scalar(SBQ2, ps[:, 6, 384:385], SCALE, None, ALU.mult).then_inc(lora_ev, 1)
            dve.wait_ge(lora_pe, 3)
            v.tensor_tensor(bo2[:], ps[:, 7, 0:C], bp[:], ALU.add).then_inc(lora_ev, 1)
            for q in range(QUARTERS):
                for w in range(2):
                    n = 2 * q + w
                    f, parts = qk[:, q % 2, w, :], qkparts[:, q % 2, w]
                    dve.wait_ge(f_done, n + 1)
                    v.tensor_tensor(f, f, parts[:, 0, :], ALU.subtract).then_inc(parts_done, 1)
                    dve.wait_ge(parts_done, 3 * n + 1)
                    v.tensor_copy(parts[:, 1, :], f).then_inc(parts_done, 1)
                    dve.wait_ge(parts_done, 3 * n + 2)
                    v.tensor_tensor(parts[:, 2, :], f, parts[:, 1, :], ALU.subtract).then_inc(parts_done, 1)

            def stacks(j, par):
                if not isinstance(j, int) or j >= 2:
                    dve.wait_ge(b_s2, j - 1)
                for e in range(2):
                    for h in range(2):
                        last = v.tensor_scalar(Q2st[0:ROWS, par, e, :, N * h:N * h + N],
                                               Qall[0:ROWS, :, bass.ds(j * 128 + N * e, N)],
                                               head_rows[0:ROWS, h:h + 1], None, ALU.mult)
                last.then_inc(b_st, 1)

            def maxima(j, par):
                dve.wait_ge(b_s1, j + 1)
                v.tensor_reduce(nmf2[:, par, :], ps[:, 0:2, :].rearrange("p e (a m) -> p (e a) m", m=N), AX.X,
                                ALU.max, negate=True).then_inc(b_chain, 1)
                dve.wait_ge(b_chain, j * 5 + 1)
                v.tensor_copy(nmp2[:, par, :, 0], nmf2[:, par, :]).then_inc(b_chain, 1)
                dve.wait_ge(b_chain, j * 5 + 2)
                v.tensor_tensor(nmf2[:, par, :], nmf2[:, par, :], nmp2[:, par, :, 0], ALU.subtract).then_inc(b_chain, 1)
                dve.wait_ge(b_chain, j * 5 + 3)
                v.tensor_copy(nmp2[:, par, :, 1], nmf2[:, par, :]).then_inc(b_chain, 1)
                dve.wait_ge(b_chain, j * 5 + 4)
                v.tensor_tensor(nmp2[:, par, :, 2], nmf2[:, par, :], nmp2[:, par, :, 1], ALU.subtract)\
                 .then_inc(b_chain, 1)

            def normalised(j, par):
                dve.wait_ge(b_av, j + 1)
                v.reciprocal(rden2, ps[:, 6, 256:512]).then_inc(b_norm, 1)
                dve.wait_ge(b_norm, j * 2 + 1)
                v.tensor_tensor(On2[:, par].rearrange("p g q -> p (g q)"), ps[:, 6, 0:256],
                                rden2, ALU.mult).then_inc(b_norm, 1)

            def residual_sum(j):
                dve.wait_ge(b_y, j + 1)
                x = x_all[:, bass.ds(j, 1), :].rearrange("p o c -> p (o c)")
                v.tensor_tensor(x, x, ps[:, 7, 0:C], ALU.add).then_inc(b_x, 1)

            dve.wait_ge(stack_in, 32 * SLOTS)
            stacks(0, 0)
            stacks(1, 1)
            maxima(0, 0)
            maxima(1, 1)
            stacks(2, 0)
            dve.wait_ge(x_b, 1)

            def pair(j, par):
                if exists(j + 2):
                    maxima(j + 2, par)
                if exists(j + 3):
                    stacks(j + 3, 1 - par)
                normalised(j, par)
                if exists(j - 1):
                    residual_sum(j - 1)

            over_pairs(dve, pair)
            residual_sum(TILES - 1)

            dve.wait_ge(b_x, TILES)
            normalise(2, xn1)
            dve.wait_ge(fw_in, 16 * 5)

            def best_two():
                dve.wait_ge(g_pe, 1)
                v.tensor_copy(gs[:].rearrange("p a b -> p (a b)"), ps[:, 4, 0:8 * TILES]).then_inc(g_chain, 1)
                dve.wait_ge(g_chain, 1)
                for m in range(TILES):
                    last = v.max(top[:, m, :], gs[:, m, :])
                last.then_inc(g_chain, 1)

            def their_experts():
                dve.wait_ge(g_chain, 2)
                for m in range(TILES):
                    last = v.max_index(topi[:, m, :], top[:, m, :], gs[:, m, :])
                last.then_inc(g_chain, 1)
                dve.wait_ge(g_chain, 3)
                v.tensor_copy(topf[:], topi[:])
                v.tensor_tensor(tw[:, 0, :], top[:, :, 1], top[:, :, 0], ALU.subtract).then_inc(g_chain, 1)

            def their_weights():
                dve.wait_ge(g_exp, 1)
                v.tensor_scalar(tw[:, 2, :], tw[:, 1, :], 1.0, None, ALU.add).then_inc(g_chain, 1)
                dve.wait_ge(g_chain, 5)
                v.reciprocal(tw[:, 2, :], tw[:, 2, :]).then_inc(g_chain, 1)
                dve.wait_ge(g_chain, 6)
                v.tensor_tensor(tw[:, 3, :], tw[:, 1, :], tw[:, 2, :], ALU.mult).then_inc(g_chain, 1)
                dve.wait_ge(g_chain, 7)

            def combine():
                experts = iota[:].unsqueeze(1).broadcast_to((128, TILES, EXPERTS))
                for k, c in enumerate((comb, comb2)):
                    last = v.tensor_tensor(c[:], experts, topf[:, :, k:k + 1].broadcast_to((128, TILES, EXPERTS)),
                                           ALU.is_equal)
                last.then_inc(g_chain, 1)
                dve.wait_ge(g_chain, 8)
                for k, c in enumerate((comb, comb2)):
                    last = v.tensor_tensor(c[:], c[:], tw[:, 2 + k, :].unsqueeze(2).broadcast_to((128, TILES, EXPERTS)),
                                           ALU.mult)
                last.then_inc(g_chain, 1)
                dve.wait_ge(g_chain, 9)
                v.tensor_tensor(comb[:], comb[:], comb2[:], ALU.add).then_inc(g_chain, 1)
                dve.wait_ge(g_chain, 10)

            def hidden(q, e, m):
                n = q * (EXPERTS * HT) + (HT * e + m)
                dve.wait_ge(h_sil, n + 1)
                if not isinstance(n, int) or n >= 2 * HT:
                    dve.wait_ge(y_pe, q * EXPERTS + e - 1)
                v.tensor_tensor(hT[:, e % 2, m, :], ps[:, 2 + m % 2, :], sil[:, m % 2, :], ALU.mult).then_inc(h_done, 1)

            def add_expert(q, e):
                n = q * EXPERTS + e
                dve.wait_ge(y_pe, n + 1)
                if isinstance(n, int):
                    wait(dve, y_done, n)
                else:
                    dve.wait_ge(y_done, n)
                for k in range(CT):
                    w = comb[:, bass.ds(q * CT + k, 1), e:e + 1].rearrange("p o e -> p (o e)")
                    before = x_all[:, bass.ds(q * CT + k, 1), :].rearrange("p o c -> p (o c)") if e == 0 else \
                        acc[:, (e + 1) % 2, k, :]
                    last = v.scalar_tensor_tensor(acc[:, e % 2, k, :], ps[:, 5 + e % 2, 128 * k:128 * k + 128], w,
                                                  before, ALU.mult, ALU.add)
                last.then_inc(y_done, 1)

            def finish(q, par):
                add_expert(q, EXPERTS - 1)
                dve.wait_ge(y_done, q * EXPERTS + EXPERTS)
                wait(dve, o_out[par], 16 * (q // 2))
                v.tensor_copy(out_t[:, par], acc[:, (EXPERTS - 1) % 2]).then_inc(o_done, 1)

            def chunk_with(q, before, par):
                for e in range(EXPERTS):
                    for m in range(HT):
                        hidden(q, e, m)
                        if q == 0 and e == 0:
                            (best_two, their_experts, their_weights, combine)[m]()
                        if m == 1:
                            if e:
                                add_expert(q, e - 1)
                            elif before is not None:
                                finish(before, par)

            for q in range(CHUNKS):
                chunk_with(q, q - 1 if q else None, (q - 1) % 2)
            finish(CHUNKS - 1, (CHUNKS - 1) % 2)


def kernel(**inputs):
    import concourse.bacc as bacc
    from concourse.bass_utils import run_bass_kernel_spmd as run

    g = {k: np.asarray(v) for k, v in inputs.items()}
    xa, at, ff = "L0_xattn_", "L0_attn_", "L0_ffn_"

    def by_pair(w):
        o = np.zeros((GP, 32, GROUPS, 2, C), w.dtype)
        w = w.reshape(GROUPS, GP, 2, D, C)
        for h in range(2):
            o[:, D * h:D * h + D, :, h, :] = w[:, :, h].transpose(1, 2, 0, 3)
        return o.reshape(128, GROUPS, 2, C)

    def by_batch(w):
        o = np.zeros((GP, 2, 2, D, GROUPS, 2, 2, C), w.dtype)
        w = w.reshape(GROUPS, GP, 2, D, C)
        for e in range(2):
            for h in range(2):
                o[:, e, h, :, :, e, h, :] = w[:, :, h].transpose(1, 2, 0, 3)
        return o.reshape(128, GROUPS, 2, 2, C)

    wqkv, bqkv = g[at + "w_qkv"], g[at + "b_qkv"].reshape(3, C, 1)
    rows = np.arange(128)
    f = np.float32
    arrays = {
        "x": g["x"].reshape(T, C), "ctxT": g["ctx_1024"].transpose(0, 2, 1),
        "WqT": g[xa + "Wq"].T, "WkT": g[xa + "Wk"].T, "WvT": g[xa + "Wv"].T, "WoP": by_pair(g[xa + "Wo"].T),
        "bq": g[xa + "bq"].reshape(C, 1), "bk": g[xa + "bk"].reshape(C, 1), "bv": np.tile(g[xa + "bv"].reshape(C, 1), (1, 128)), "WoT": g[xa + "Wo"].T,
        "wqT": wqkv[:, 0:C].T, "wk": wqkv[:, C:2 * C], "wvT": wqkv[:, 2 * C:].T,
        "sbq": bqkv[0], "sbk": bqkv[1], "sbv": np.tile(bqkv[2], (1, 128)),
        "aqT": np.tile(g[at + "a_q"].T, (1, H)), "bbq": np.tile(g[at + "b_q"], (1, H)),
        "avT": np.tile(g[at + "a_v"].T, (1, H)), "bbv": np.tile(g[at + "b_v"], (1, H)),
        "Wp": g[at + "w_proj"], "WpE": by_batch(g[at + "w_proj"]),
        "batch_ones": (rows[:, None] // N == np.arange(VS) // (2 * D)).astype(f), "bp": g[at + "b_proj"].reshape(1, C),
        "gateT": g[ff + "gate_w"].T, "W1T": g[ff + "w1"].transpose(2, 0, 1), "W3T": g[ff + "w3"].transpose(2, 0, 1),
        "W2T": g[ff + "w2"].transpose(2, 0, 1).reshape(HT, 128, EXPERTS, C).transpose(1, 2, 0, 3),
        "ident": np.eye(128, dtype=f), "head_rows": (rows[:, None] // D % 2 == np.arange(2)).astype(f),
        "head_block": (rows[:, None] // D == rows // D).astype(f),
        "iota": np.tile(np.arange(EXPERTS, dtype=f), (128, 1)),
    }
    nc = bacc.Bacc("TRN2", target_bir_lowering=False, num_devices=1)
    t = {}
    for name, shape in INS.items():
        arrays[name] = np.ascontiguousarray(arrays[name])
        assert arrays[name].shape == shape, name
        t[name] = nc.dram_tensor("in_" + name, shape, F32, kind="ExternalInput").ap()
    out = nc.dram_tensor("out", (T, C), F32, kind="ExternalOutput").ap()
    perceiver(nc, t, out)
    r = run(nc, [{"in_" + n: a for n, a in arrays.items()}], core_ids=[0])
    return r.results[0]["out"].reshape(B, N, C)
```
